# Optimizing a Trainium2 kernel written in Bass

```python
import numpy as np
import jax
import jax.numpy as jnp

def _softmax(x, axis=-1):
    return jax.nn.softmax(x, axis=axis)

def _gelu(x):
    return jax.nn.gelu(x, approximate=True)

def _silu(x):
    return jax.nn.silu(x)

def _sigmoid(x):
    return jax.nn.sigmoid(x)

def _layernorm(x, axis=-1, eps=1e-05):
    m = jnp.mean(x, axis=axis, keepdims=True)
    v = jnp.var(x, axis=axis, keepdims=True)
    return (x - m) / jnp.sqrt(v + eps)

def _scatter_add(tgt, idx, src, axis=0):
    return tgt.at[idx].add(src)

def _segment_sum(src, seg, n):
    return jax.ops.segment_sum(src, seg, n)
kernel_name = 'mk_early_fusion_d1_tok_img1024_r4_2694e1'

def setup_inputs(seed: int=0):
    np.random.seed(seed)
    _w = jnp.asarray

    def _rec_inputs():
        import jax
        import jax.numpy as jnp
        _rk = jax.random.key(seed)
        x = -0.000222058 + 0.999998 * jax.random.normal(jax.random.fold_in(_rk, 1), (8, 128, 128, 3), jnp.float32)
        txt = -0.000342796 + 1.00012 * jax.random.normal(jax.random.fold_in(_rk, 2), (8, 128, 256), jnp.float32)
        return (x, txt)
    x, txt = _rec_inputs()

    def _L0_tok_setup():
        import jax, jax.numpy as jnp
        import numpy as np
        PATCH = 16
        CHANNELS = 3
        HIDDEN = 256
        key = jax.random.key(seed)
        k1, k2 = jax.random.split(key)
        inputs = jax.random.normal(k1, (32, 128, 128, 3), dtype=jnp.float32)
        fan_in = CHANNELS * PATCH * PATCH
        W = jax.random.normal(k2, (fan_in, HIDDEN), dtype=jnp.float32) / np.sqrt(fan_in)
        return {'inputs': inputs, 'W': W}
    _L0_tok_all = _L0_tok_setup()
    _L0_tok_in = {k: v for k, v in _L0_tok_all.items() if k in ('W',)}
    del _L0_tok_all

    def _L0_attn_setup():
        import jax, jax.numpy as jnp
        import numpy as np
        DIM = 256
        NUM_HEADS = 16
        HEAD_DIM = DIM // NUM_HEADS
        TAU = 2.0
        V_TH = 1.0
        BN_EPS = 1e-05

        def _branch(x, W, gamma, beta):
            B, N, D = x.shape
            h = jnp.einsum('bnd,ed->bne', x, W)
            hf = h.reshape(B * N, D)
            mean = jnp.mean(hf, axis=0)
            var = jnp.var(hf, axis=0)
            hn = (hf - mean) * jax.lax.rsqrt(var + BN_EPS) * gamma + beta
            hn = hn.reshape(B, N, D)
            return jax.nn.sigmoid(4.0 * (hn - V_TH))

        def _heads(x):
            B, N, D = x.shape
            return x.reshape(B, N, NUM_HEADS, HEAD_DIM).transpose(0, 2, 1, 3)
        key = jax.random.key(seed)
        ks = jax.random.split(key, 12)
        B, N, D = (8, 1024, DIM)
        s = 0.02
        return {'x': jax.random.normal(ks[0], (B, N, D), dtype=jnp.float32), 'Wq': jax.random.normal(ks[1], (D, D), dtype=jnp.float32) * s, 'gq': jnp.ones((D,), jnp.float32), 'bq': jnp.zeros((D,), jnp.float32), 'Wk': jax.random.normal(ks[2], (D, D), dtype=jnp.float32) * s, 'gk': jnp.ones((D,), jnp.float32), 'bk': jnp.zeros((D,), jnp.float32), 'Wv': jax.random.normal(ks[3], (D, D), dtype=jnp.float32) * s, 'gv': jnp.ones((D,), jnp.float32), 'bv': jnp.zeros((D,), jnp.float32), 'Wp': jax.random.normal(ks[4], (D, D), dtype=jnp.float32) * s, 'bp': jnp.zeros((D,), jnp.float32)}
    _L0_attn_all = _L0_attn_setup()
    _L0_attn_in = {k: v for k, v in _L0_attn_all.items() if k in ('Wq', 'gq', 'bq', 'Wk', 'gk', 'bk', 'Wv', 'gv', 'bv', 'Wp', 'bp')}
    del _L0_attn_all

    def _L0_ffn_setup():
        import jax, jax.numpy as jnp
        import numpy as np
        EPS = 1e-06
        LN_EPS = 1e-05

        def _absmean_core(W):
            gamma = jnp.mean(jnp.abs(W)) + EPS
            Ws = W / gamma
            Wq = jnp.sign(Ws) * jnp.minimum(jnp.round(jnp.abs(Ws)), 1.0)
            return (Wq, gamma)

        @jax.custom_vjp
        def absmean(W):
            return _absmean_core(W)[0]

        def _absmean_fwd(W):
            Wq, gamma = _absmean_core(W)
            return (Wq, gamma)

        def _absmean_bwd(gamma, g):
            return (g / gamma,)
        absmean.defvjp(_absmean_fwd, _absmean_bwd)

        def layernorm(x, w, b, eps=LN_EPS):
            mu = jnp.mean(x, axis=-1, keepdims=True)
            var = jnp.mean((x - mu) ** 2, axis=-1, keepdims=True)
            return (x - mu) * jax.lax.rsqrt(var + eps) * w + b
        key = jax.random.key(seed)
        k1, k2, k3 = jax.random.split(key, 3)
        d, h = (256, 1024)
        B, T = (8, 512)
        return {'x': jax.random.normal(k1, (B, T, d), jnp.float32), 'W_fc': jax.random.normal(k2, (h, d), jnp.float32), 'ln_w': jnp.ones((h,), jnp.float32), 'ln_b': jnp.zeros((h,), jnp.float32), 'W_proj': jax.random.normal(k3, (d, h), jnp.float32)}
    _L0_ffn_all = _L0_ffn_setup()
    _L0_ffn_in = {k: v for k, v in _L0_ffn_all.items() if k in ('W_fc', 'ln_w', 'ln_b', 'W_proj')}
    del _L0_ffn_all
    return {'x': x, 'txt': txt, 'L0_tok_W': _L0_tok_in['W'], 'L0_attn_Wq': _L0_attn_in['Wq'], 'L0_attn_gq': _L0_attn_in['gq'], 'L0_attn_bq': _L0_attn_in['bq'], 'L0_attn_Wk': _L0_attn_in['Wk'], 'L0_attn_gk': _L0_attn_in['gk'], 'L0_attn_bk': _L0_attn_in['bk'], 'L0_attn_Wv': _L0_attn_in['Wv'], 'L0_attn_gv': _L0_attn_in['gv'], 'L0_attn_bv': _L0_attn_in['bv'], 'L0_attn_Wp': _L0_attn_in['Wp'], 'L0_attn_bp': _L0_attn_in['bp'], 'L0_ffn_W_fc': _L0_ffn_in['W_fc'], 'L0_ffn_ln_w': _L0_ffn_in['ln_w'], 'L0_ffn_ln_b': _L0_ffn_in['ln_b'], 'L0_ffn_W_proj': _L0_ffn_in['W_proj']}

def reference(x, txt, L0_tok_W, L0_attn_Wq, L0_attn_gq, L0_attn_bq, L0_attn_Wk, L0_attn_gk, L0_attn_bk, L0_attn_Wv, L0_attn_gv, L0_attn_bv, L0_attn_Wp, L0_attn_bp, L0_ffn_W_fc, L0_ffn_ln_w, L0_ffn_ln_b, L0_ffn_W_proj):
    import jax
    import jax.numpy as jnp

    def _L0_tok_ref(inputs, W):
        import jax, jax.numpy as jnp
        import numpy as np
        PATCH = 16
        CHANNELS = 3
        HIDDEN = 256
        if inputs.shape[1] == CHANNELS and inputs.shape[-1] != CHANNELS:
            inputs = jnp.transpose(inputs, (0, 2, 3, 1))
        b, h, w, c = inputs.shape
        p = PATCH
        patches = inputs.reshape(b, h // p, p, w // p, p, c)
        patches = jnp.transpose(patches, (0, 1, 3, 2, 4, 5))
        patches = patches.reshape(b, -1, p * p * c)
        return jnp.einsum('bnf,fh->bnh', patches, W)

    def _L0_attn_ref(x, Wq, gq, bq, Wk, gk, bk, Wv, gv, bv, Wp, bp):
        import jax, jax.numpy as jnp
        import numpy as np
        DIM = 256
        NUM_HEADS = 16
        HEAD_DIM = DIM // NUM_HEADS
        TAU = 2.0
        V_TH = 1.0
        BN_EPS = 1e-05

        def _branch(x, W, gamma, beta):
            B, N, D = x.shape
            h = jnp.einsum('bnd,ed->bne', x, W)
            hf = h.reshape(B * N, D)
            mean = jnp.mean(hf, axis=0)
            var = jnp.var(hf, axis=0)
            hn = (hf - mean) * jax.lax.rsqrt(var + BN_EPS) * gamma + beta
            hn = hn.reshape(B, N, D)
            return jax.nn.sigmoid(4.0 * (hn - V_TH))

        def _heads(x):
            B, N, D = x.shape
            return x.reshape(B, N, NUM_HEADS, HEAD_DIM).transpose(0, 2, 1, 3)
        B, N, D = x.shape
        scale = HEAD_DIM ** (-0.5)
        q = _branch(x, Wq, gq, bq)
        k = _branch(x, Wk, gk, bk)
        v = _branch(x, Wv, gv, bv)
        qk = _heads(q * k) * scale
        v_h = _heads(v)
        vv = jnp.einsum('bhnd,bhne->bhde', v_h, v_h)
        out = jnp.einsum('bhnd,bhde->bhne', qk, vv)
        out = out.transpose(0, 2, 1, 3).reshape(B, N, D)
        return jnp.einsum('bnd,ed->bne', out, Wp) + bp

    def _L0_ffn_ref(x, W_fc, ln_w, ln_b, W_proj):
        import jax, jax.numpy as jnp
        import numpy as np
        EPS = 1e-06
        LN_EPS = 1e-05

        def _absmean_core(W):
            gamma = jnp.mean(jnp.abs(W)) + EPS
            Ws = W / gamma
            Wq = jnp.sign(Ws) * jnp.minimum(jnp.round(jnp.abs(Ws)), 1.0)
            return (Wq, gamma)

        @jax.custom_vjp
        def absmean(W):
            return _absmean_core(W)[0]

        def _absmean_fwd(W):
            Wq, gamma = _absmean_core(W)
            return (Wq, gamma)

        def _absmean_bwd(gamma, g):
            return (g / gamma,)
        absmean.defvjp(_absmean_fwd, _absmean_bwd)

        def layernorm(x, w, b, eps=LN_EPS):
            mu = jnp.mean(x, axis=-1, keepdims=True)
            var = jnp.mean((x - mu) ** 2, axis=-1, keepdims=True)
            return (x - mu) * jax.lax.rsqrt(var + eps) * w + b
        h = jnp.einsum('btd,hd->bth', x, absmean(W_fc))
        h = jax.nn.gelu(h, approximate=False)
        h = layernorm(h, ln_w, ln_b)
        return jnp.einsum('bth,dh->btd', h, absmean(W_proj))
    h = _L0_tok_ref(x, L0_tok_W)
    h = jnp.concatenate([h, txt], axis=1)
    h = h + _L0_attn_ref(_layernorm(h, axis=-1), L0_attn_Wq, L0_attn_gq, L0_attn_bq, L0_attn_Wk, L0_attn_gk, L0_attn_bk, L0_attn_Wv, L0_attn_gv, L0_attn_bv, L0_attn_Wp, L0_attn_bp)
    h = h + _L0_ffn_ref(_layernorm(h, axis=-1), L0_ffn_W_fc, L0_ffn_ln_w, L0_ffn_ln_b, L0_ffn_W_proj)
    return h

_drawn_inputs = setup_inputs


def setup_inputs(seed=0):
    import zlib

    import numpy as np

    out = dict(_drawn_inputs(seed))
    spreads = {'L0_attn_gq': (1.0, 0.2),
     'L0_attn_bq': (0.0, 0.1),
     'L0_attn_gk': (1.0, 0.2),
     'L0_attn_bk': (0.0, 0.1),
     'L0_attn_gv': (1.0, 0.2),
     'L0_attn_bv': (0.0, 0.1),
     'L0_attn_bp': (0.0, 0.1),
     'L0_ffn_ln_w': (1.0, 0.2),
     'L0_ffn_ln_b': (0.0, 0.1)}
    factors = {}
    for name, (base, spread) in spreads.items():
        noise = np.random.default_rng([zlib.crc32(name.encode()), seed]).standard_normal(out[name].shape)
        drawn = base * np.exp(spread * noise) if base else spread * noise
        out[name] = jnp.asarray(drawn.astype(out[name].dtype))
    for name, factor in factors.items():
        out[name] = (out[name] * factor).astype(out[name].dtype)
    return out
```

```python
import numpy as np
import concourse.bass as bass
from concourse import mybir
from contextlib import ExitStack

P = 128
BATCHES, IMAGE_TOKENS, TEXT_TOKENS = 8, 64, 128
DIM, HEADS, HIDDEN = 256, 16, 1024
HEAD_DIM = DIM // HEADS
PATCH = 16
PATCH_FEATURES = 3 * PATCH * PATCH
TOKENS = BATCHES * (IMAGE_TOKENS + TEXT_TOKENS)
TILES = TOKENS // P
IMAGE_TILES = BATCHES * IMAGE_TOKENS // P
GROUP_TILES = 4
GROUP = GROUP_TILES * P
GROUPS = TILES // GROUP_TILES
DIM_CHUNKS = DIM // P
HIDDEN_CHUNKS = HIDDEN // P
PATCH_CHUNKS = PATCH_FEATURES // P
NORM_EPS = 1e-5
ABSMEAN_EPS = 1e-6
V_THRESHOLD, SIGMOID_SLOPE = 1.0, 4.0
V, K, Q = 0, 1, 2

GROUP_ORDER = (1, 2, 0)


def bank_uses():
    uses = []

    def use(what, bank):
        uses.append((what, bank))

    for n, (g, k) in enumerate([(1, 0), (1, 1), (2, 0), (2, 1)]):
        use(("xnT", k, g), n)
    for (m, c, g), bank in {(V, 0, 1): 4, (V, 0, 2): 5, (V, 1, 1): 6, (V, 1, 2): 7, (K, 0, 1): 0, (K, 0, 2): 1}.items():
        use(("qkv", m, c, g), bank)
    for t in range(IMAGE_TILES):
        use(("embed", t), 2 + t % 2)
    use(("xnT", 0, 0), 2)
    use(("xnT", 1, 0), 3)
    use(("qkv", V, 0, 0), 2)
    use(("qkv", V, 1, 0), 3)
    use(("qkv", K, 0, 0), 4)
    use(("absmean",), 7)
    use(("qkv", K, 1, 1), 5)
    use(("qkv", K, 1, 2), 2)
    for n, g in enumerate(GROUP_ORDER):
        use(("valueT", 0, g), (7, 3)[n % 2])
    use(("qkv", K, 1, 0), 6)
    for n, g in enumerate(GROUP_ORDER):
        use(("valueT", 1, g), (3, 7)[n % 2])
    for half in range(2):
        use(("gram", 0, half), (7, 3)[half])
    for g, bank in zip(GROUP_ORDER, (0, 1, 4)):
        use(("qkv", Q, 0, g), bank)
    for half in range(2):
        use(("gram", 1, half), (7, 3)[half])
    for g, bank in zip(GROUP_ORDER, (5, 2, 6)):
        use(("qkv", Q, 1, g), bank)
    use(("ffn_rows",), 7)
    for g, bank in zip(GROUP_ORDER, (3, 0, 1)):
        use(("mix", 0, g), bank)
    for g, bank in zip(GROUP_ORDER, (4, 5, 4)):
        use(("mix", 1, g), bank)
    return uses


def block(
    nc, patches_in, text_in, w_embed_in, w_qkv_in, w_proj_in, w_up_in, w_down_in,
    columns_in, proj_bias_in, squares_in, out,
):
    fp32, fp32r = mybir.dt.float32, mybir.dt.float32r
    ALU, ACT = mybir.AluOpType, mybir.ActivationFunctionType

    with ExitStack() as ctx:
        def sem(name):
            return ctx.enter_context(nc.semaphore(name))

        offset = [nc.sbuf_base]
        floats = 4

        def place(name, shape, dt=fp32, at=None):
            size = int(np.prod(shape[1:])) * floats
            if at is None:
                at = -(-offset[0] // 32) * 32
                offset[0] = at + size
            return nc.alloc_sbuf_tensor_at(name, shape, dt, offset=at), at, at + size

        h, _, _ = place("h", [P, TILES, DIM])
        xn, _, _ = place("xn", [P, TILES, DIM])
        xnT_hi, at_xnT, _ = place("xnT_hi", [P, DIM_CHUNKS, TOKENS], fp32r)
        xnT_lo, at_xnT_lo, _ = place("xnT_lo", [P, DIM_CHUNKS, TOKENS], fp32r)
        attT_hi, _, _ = place("attT_hi", [P, DIM_CHUNKS, TOKENS], fp32r, at_xnT)
        attT_lo, _, _ = place("attT_lo", [P, DIM_CHUNKS, TOKENS], fp32r, at_xnT_lo)
        x2T_hi, at_x2T, _ = place("x2T_hi", [P, DIM_CHUNKS, TOKENS], fp32r)
        x2T_low, _, _ = place("x2T_low", [P, DIM_CHUNKS, TOKENS], fp32r)
        patches, _, after = place("patches", [P, PATCH_CHUNKS, GROUP], fp32, at_x2T)
        w_embed, _, _ = place("w_embed", [P, PATCH_CHUNKS, DIM], fp32, after)
        act_qkv, at_qkv, _ = place("act_qkv", [P, 3 * DIM_CHUNKS, TOKENS])
        gT_hi, _, after = place("gT_hi", [P, HIDDEN_CHUNKS, GROUP], fp32r, at_qkv)
        gT_lo, _, _ = place("gT_lo", [P, HIDDEN_CHUNKS, GROUP], fp32r, after)
        g, at_g, _ = place("g", [P, 2 * GROUP_TILES, HIDDEN])
        v_text, _, after = place("v_text", [P, DIM_CHUNKS, BATCHES, P], fp32, at_g)
        v_image, _, after = place("v_image", [P, DIM_CHUNKS, 2, IMAGE_TILES, P], fp32, after)
        gram, _, after = place("gram", [P, DIM_CHUNKS, BATCHES, P], fp32, after)
        w_qkv, _, after = place("w_qkv", [P, DIM_CHUNKS, 3 * DIM], fp32, after)
        w_proj, _, _ = place("w_proj", [P, DIM_CHUNKS, DIM], fp32, after)
        w_qkv_hi, _, _ = place("w_qkv_hi", [P, DIM_CHUNKS, 3 * DIM], fp32r)
        w_qkv_lo, _, _ = place("w_qkv_lo", [P, DIM_CHUNKS, 3 * DIM], fp32r)
        w_proj_hi, _, _ = place("w_proj_hi", [P, DIM_CHUNKS, DIM], fp32r)
        w_proj_lo, _, _ = place("w_proj_lo", [P, DIM_CHUNKS, DIM], fp32r)
        w_up, _, _ = place("w_up", [P, DIM_CHUNKS * HIDDEN])
        w_down, _, _ = place("w_down", [P, HIDDEN_CHUNKS * DIM])
        up_sign, _, _ = place("up_sign", [P, DIM_CHUNKS * HIDDEN], fp32r)
        down_sign, _, _ = place("down_sign", [P, HIDDEN_CHUNKS * DIM], fp32r)
        up_negative, _, after = place("up_negative", [P, DIM_CHUNKS * HIDDEN], fp32, at_x2T)
        negative, _, after = place("negative", [P, 512], fp32, after)
        positive, _, _ = place("positive", [P, 512], fp32, after)
        squares, _, _ = place("squares", [P, 2 * P])
        columns, _, _ = place("columns", [P, 30])
        proj_bias, _, _ = place("proj_bias", [P, DIM])
        ones, _, _ = place("ones", [P, P])
        minus_half, _, _ = place("minus_half", [P, GROUP_TILES])
        rows, _, _ = place("rows", [P, 2, DIM])
        row_weights_hi, _, _ = place("row_weights_hi", [P, 2 * HIDDEN_CHUNKS], fp32r)
        row_weights_lo, _, _ = place("row_weights_lo", [P, 2 * HIDDEN_CHUNKS], fp32r)
        norm_stats, _, _ = place("norm_stats", [P, 2, TILES, 6])
        norm_moments, _, _ = place("norm_moments", [P, 2, TILES, 2])
        norm_var, _, _ = place("norm_var", [P, 2, TILES])
        norm_rstd, _, _ = place("norm_rstd", [P, 2, TILES])
        bn_stats, _, _ = place("bn_stats", [P, 3 * DIM_CHUNKS, GROUPS * 6])
        bn_moments, _, _ = place("bn_moments", [P, 3 * DIM_CHUNKS, 2])
        bn_var, _, _ = place("bn_var", [P, 3 * DIM_CHUNKS])
        bn_rstd, _, _ = place("bn_rstd", [P, 3 * DIM_CHUNKS])
        bn_slope, _, _ = place("bn_slope", [P, 3 * DIM_CHUNKS])
        bn_minus_slope, _, _ = place("bn_minus_slope", [P, 3 * DIM_CHUNKS])
        bn_shift, _, _ = place("bn_shift", [P, 3 * DIM_CHUNKS])
        g_stats, _, _ = place("g_stats", [P, TILES, 2, 6])
        g_moments, _, _ = place("g_moments", [P, TILES, 2])
        g_var, _, _ = place("g_var", [P, TILES])
        g_rstd, _, _ = place("g_rstd", [P, TILES])
        g_minus_mean, _, _ = place("g_minus_mean", [P, TILES])
        abs_sums, _, _ = place("abs_sums", [P, 2])
        absmeans, _, _ = place("absmeans", [P, 2])
        thresholds, _, _ = place("thresholds", [P, 2, 2])
        final, _, _ = place("final", [P, 2, DIM])

        identity, head_mask = squares[:, 0:P], squares[:, P:2 * P]
        gain4 = columns[:, 0:6]
        shift = columns[:, 6:12]
        ln_w, ln_b = columns[:, 12:20], columns[:, 20:28]
        half_mask = (columns[:, 28:29], columns[:, 29:30])
        bn_gain, _, _ = place("bn_gain", [P, 6])
        bn_minus_gain, _, _ = place("bn_minus_gain", [P, 6])
        bn_offset, _, _ = place("bn_offset", [P, 6])
        assert offset[0] <= nc.sbuf_usable_end, offset[0]

        psum = ctx.enter_context(nc.psum_tensor("psum", [P, 8, 512], fp32))

        USES = bank_uses()
        order = GROUP_ORDER

        def tiles_of(group):
            return range(GROUP_TILES * group, GROUP_TILES * (group + 1))

        gt_bank = [0]

        def use(what, bank):
            USES.append((what, bank))

        def proj_uses(s):
            for pair in range(2):
                use(("proj", 2 * (2 * order[s] + pair)), 6 + pair)

        def x2T_uses(s):
            for k in range(DIM_CHUNKS):
                use(("x2T", k, order[s]), 4 + k)

        def up_use(s, i):
            use(("up", GROUP_TILES * order[s] + i), 2 * (i % 2))

        def gT_use(s, c):
            use(("gT", c, order[s]), 4 + c % 2)

        def down_use(s, i):
            use(("down", GROUP_TILES * order[s] + i), 6 + i % 2)

        proj_uses(0)
        proj_uses(1)
        x2T_uses(0)
        for i in range(GROUP_TILES):
            up_use(0, i)
        proj_uses(2)
        x2T_uses(1)
        for s in range(1, GROUPS):
            for i in range(GROUP_TILES):
                gT_use(s - 1, 2 * i)
                gT_use(s - 1, 2 * i + 1)
                up_use(s, i)
            if s + 1 < GROUPS:
                x2T_uses(s + 1)
            for i in range(GROUP_TILES):
                down_use(s - 1, i)
        LAST_DOWN_BANKS = (0, 1, 2, 3)
        for c in range(HIDDEN_CHUNKS):
            gT_use(GROUPS - 1, c)

        nth, BANK, BEFORE = {}, {}, {}
        held = [[] for _ in range(8)]

        def hold(what, bank):
            BEFORE[what] = held[bank][-1] if held[bank] else None
            held[bank].append(what)
            nth[what], BANK[what] = len(held[bank]), bank

        for what, bank in USES:
            hold(what, bank)
            if what[0] == "up":
                hold(("up2", what[1]), bank + 1)
        for i, bank in enumerate(LAST_DOWN_BANKS):
            hold(("down", GROUP_TILES * order[-1] + i), bank)

        bank_full = [sem(f"bank_full{b}") for b in range(8)]

        text_loaded = [sem("text_loaded_g1"), sem("text_loaded_g2")]
        w_qkv_loaded = sem("w_qkv_loaded")
        constants_loaded = sem("constants_loaded")
        patches_loaded = sem("patches_loaded")
        w_proj_loaded = sem("w_proj_loaded")
        w_up_loaded = sem("w_up_loaded")
        w_down_loaded = sem("w_down_loaded")
        out_stored = sem("out_stored")
        w_qkv_hi_ready, w_qkv_lo_ready = sem("w_qkv_hi_ready"), sem("w_qkv_lo_ready")
        w_proj_hi_ready, w_proj_lo_ready = sem("w_proj_hi_ready"), sem("w_proj_lo_ready")
        pool_constants = sem("pool_constants")
        norm_stat, norm_moment = sem("norm_stat"), sem("norm_moment")
        norm_var_ready, norm_rstd_ready = sem("norm_var_ready"), sem("norm_rstd_ready")
        xn_ready = sem("xn_ready")
        xT_hi_ready, xT_lo_ready = sem("xT_hi_ready"), sem("xT_lo_ready")
        bn_constants = sem("bn_constants")
        bn_stat, bn_moment = sem("bn_stat"), sem("bn_moment")
        bn_var_ready, bn_rstd_ready = sem("bn_var_ready"), sem("bn_rstd_ready")
        bn_slopes, bn_ready = sem("bn_slopes"), sem("bn_ready")
        sigmoid_ready = sem("sigmoid_ready")
        abs_ready, absmean_ready, threshold_ready = sem("abs_ready"), sem("absmean_ready"), sem("threshold_ready")
        up_part, down_part = sem("up_part"), sem("down_part")
        up_ready, down_ready = sem("up_ready"), sem("down_ready")
        value_ready, gram_ready = sem("value_ready"), sem("gram_ready")
        qk0_ready, qk1_ready = sem("qk0_ready"), sem("qk1_ready")
        att_hi_ready, att_lo_ready = sem("att_hi_ready"), sem("att_lo_ready")
        embed_ready, biased = sem("embed_ready"), sem("biased")
        h2_ready, h2_shifted = sem("h2_ready"), sem("h2_shifted")
        row_weight_hi_ready, row_weight_ready = sem("row_weight_hi_ready"), sem("row_weight_ready")
        rows_ready = sem("rows_ready")
        g_ready = sem("g_ready")
        g_stat, g_moment = sem("g_stat"), sem("g_moment")
        g_var_ready, g_rstd_ready, g_mean_ready = sem("g_var_ready"), sem("g_rstd_ready"), sem("g_mean_ready")
        gT_hi_ready, gT_lo_ready = sem("gT_hi_ready"), sem("gT_lo_ready")
        final_part, final_ready = sem("final_part"), sem("final_ready")
        final_order = [GROUP_TILES * gr + i for gr in order for i in range(GROUP_TILES)]

        def place_of(t):
            return GROUP_TILES * order.index(t // GROUP_TILES) + t % GROUP_TILES

        def was_read(what):
            kind, *at = what
            if kind == "xnT":
                k, group = at
                return xT_lo_ready, DIM_CHUNKS * order.index(group) + k + 1
            if kind == "x2T":
                k, group = at
                return xT_lo_ready, DIM_CHUNKS * (GROUPS + order.index(group)) + k + 1
            if kind == "embed":
                return embed_ready, at[0] + 1
            if kind == "qkv":
                m, c, group = at
                return sigmoid_ready, GROUPS * (DIM_CHUNKS * m + c) + order.index(group) + 1
            if kind == "absmean":
                return absmean_ready, 1
            if kind == "valueT":
                c, group = at
                return value_ready, GROUPS * c + order.index(group) + 1
            if kind == "gram":
                c, half = at
                return gram_ready, 2 * c + half + 1
            if kind == "ffn_rows":
                return rows_ready, 1
            if kind == "mix":
                c, group = at
                return att_lo_ready, GROUPS * c + order.index(group) + 1
            if kind == "proj":
                return h2_ready, place_of(at[0]) // 2 + 1
            if kind in ("up", "up2"):
                return g_ready, place_of(at[0]) + 1
            if kind == "gT":
                c, group = at
                return gT_lo_ready, HIDDEN_CHUNKS * order.index(group) + c + 1
            return final_part, place_of(at[0]) + 1

        def cols(group):
            return slice(GROUP * group, GROUP * (group + 1))

        def qkv_index(m, c):
            return DIM_CHUNKS * m + c

        blk = ctx.enter_context(nc.Block())

        @blk.sync
        def _(sp):
            sp.dma_start(h[:, 4:8, :], text_in[:, 0:4, :]).then_inc(text_loaded[0], 16)
            sp.dma_start(h[:, 8:12, :], text_in[:, 4:8, :]).then_inc(text_loaded[1], 16)
            sp.dma_start(w_qkv[:, :, :], w_qkv_in).then_inc(w_qkv_loaded, 16)
            sp.dma_start(squares[:, :], squares_in).then_inc(constants_loaded, 16)
            sp.dma_start(columns[:, :], columns_in).then_inc(constants_loaded, 16)
            sp.dma_start(proj_bias[:, :], proj_bias_in.partition_broadcast(P)).then_inc(constants_loaded, 16)
            sp.dma_start(w_embed[:, :, :], w_embed_in).then_inc(patches_loaded, 16)
            sp.dma_start(patches[:, :, :], patches_in).then_inc(patches_loaded, 16)
            sp.dma_start(w_up[:, :], w_up_in).then_inc(w_up_loaded, 16)
            sp.dma_start(w_down[:, :], w_down_in).then_inc(w_down_loaded, 16)
            sp.dma_start(w_proj[:, :, :], w_proj_in).then_inc(w_proj_loaded, 16)
            for n, t in enumerate(final_order):
                sp.wait_ge(final_ready, n + 1)
                sp.dma_start(out[t], h[:, t, :]).then_inc(out_stored, 16)
            sp.wait_ge(out_stored, 16 * TILES)

        @blk.tensor
        def _(pe):
            def claim(what):
                if BEFORE[what]:
                    pe.wait_ge(*was_read(BEFORE[what]))
                return psum[:, BANK[what], :]

            def matmuls(dst, pairs):
                for i, (stationary, moving) in enumerate(pairs):
                    last = pe.matmul(dst, stationary, moving, start=(i == 0), stop=(i == len(pairs) - 1))
                return last

            def transposes(what, sources):
                bank = claim(what)
                for i, source in enumerate(sources):
                    last = pe.transpose(bank[:, P * i:P * (i + 1)], source, identity)
                last.then_inc(bank_full[BANK[what]], 1)

            def transpose_xn(kind, k, group):
                transposes((kind, k, group), [xn[:, t, P * k:P * (k + 1)] for t in tiles_of(group)])

            def qkv(m, c, group):
                what = ("qkv", m, c, group)
                bank = claim(what)
                e = slice(DIM * m + P * c, DIM * m + P * (c + 1))
                pairs = []
                for k in range(DIM_CHUNKS):
                    pairs += [(w_qkv_hi[:, k, e], xnT_hi[:, k, cols(group)]),
                              (w_qkv_hi[:, k, e], xnT_lo[:, k, cols(group)]),
                              (w_qkv_lo[:, k, e], xnT_hi[:, k, cols(group)])]
                matmuls(bank, pairs).then_inc(bank_full[BANK[what]], 1)

            def value_transpose(c, group):
                pe.wait_ge(sigmoid_ready, GROUPS * c + order.index(group) + 1)
                transposes(("valueT", c, group),
                           [act_qkv[:, qkv_index(V, c), P * t:P * (t + 1)] for t in tiles_of(group)])

            def gram_product(c, half):
                what = ("gram", c, half)
                bank = claim(what)
                pe.wait_ge(value_ready, GROUPS * (c + 1))
                for i in range(4):
                    b = 4 * half + i
                    vt, vi = v_text[:, c, b, :], v_image[:, c, b % 2, b // 2, :]
                    last = matmuls(bank[:, P * i:P * (i + 1)], [(vt, vt), (vi, vi)])
                last.then_inc(bank_full[BANK[what]], 1)

            def mix(c, group):
                what = ("mix", c, group)
                bank = claim(what)
                qk = act_qkv[:, qkv_index(Q, c), :]
                if group:
                    batches, width, first = range(4 * (group - 1), 4 * group), TEXT_TOKENS, GROUP * group
                else:
                    batches, width, first = range(BATCHES), IMAGE_TOKENS, 0
                pe.wait_ge((qk0_ready, qk1_ready)[c], order.index(group) + 1)
                for i, b in enumerate(batches):
                    last = pe.matmul(bank[:, width * i:width * (i + 1)], gram[:, c, b, :],
                                     qk[:, first + width * i:first + width * (i + 1)], start=True, stop=True)
                last.then_inc(bank_full[BANK[what]], 1)

            def proj(s, pair):
                t0 = GROUP_TILES * order[s] + 2 * pair
                what = ("proj", t0)
                bank = claim(what)
                for i in range(2):
                    at = slice(P * (t0 + i), P * (t0 + i + 1))
                    pairs = []
                    for c in range(DIM_CHUNKS):
                        pairs += [(attT_hi[:, c, at], w_proj_hi[:, c, :]),
                                  (attT_hi[:, c, at], w_proj_lo[:, c, :]),
                                  (attT_lo[:, c, at], w_proj_hi[:, c, :])]
                    last = matmuls(bank[:, DIM * i:DIM * (i + 1)], pairs)
                last.then_inc(bank_full[BANK[what]], 1)

            def up(t):
                claim(("up", t))
                claim(("up2", t))
                at = slice(P * t, P * (t + 1))
                for half in range(2):
                    pairs = []
                    for k in range(DIM_CHUNKS):
                        w = up_sign[:, HIDDEN * k + 512 * half:HIDDEN * k + 512 * (half + 1)]
                        pairs += [(x2T_hi[:, k, at], w), (x2T_low[:, k, at], w)]
                    matmuls(psum[:, BANK[("up", t)] + half, :], pairs).then_inc(bank_full[BANK[("up", t)] + half], 1)

            def gT(s, c):
                transposes(("gT", c, order[s]),
                           [g[:, GROUP_TILES * (s % 2) + i, P * c:P * (c + 1)] for i in range(GROUP_TILES)])

            def down_pairs(i, c):
                w = down_sign[:, DIM * c:DIM * (c + 1)]
                at = slice(P * i, P * (i + 1))
                return [(gT_hi[:, c, at], w), (gT_lo[:, c, at], w)]

            def down(s, i):
                what = ("down", GROUP_TILES * order[s] + i)
                bank = claim(what)
                matmuls(bank[:, 0:DIM], [p for c in range(HIDDEN_CHUNKS) for p in down_pairs(i, c)])\
                    .then_inc(bank_full[BANK[what]], 1)

            pe.wait_ge(constants_loaded, 48)
            for n, group in enumerate((1, 2)):
                pe.wait_ge(xn_ready, GROUP_TILES * (n + 1))
                for k in range(DIM_CHUNKS):
                    transpose_xn("xnT", k, group)
            for c in range(DIM_CHUNKS):
                for n, group in enumerate((1, 2)):
                    pe.wait_ge(w_qkv_lo_ready, 1)
                    pe.wait_ge(xT_lo_ready, 2 * (n + 1))
                    qkv(V, c, group)
            pe.wait_ge(w_qkv_lo_ready, 2)
            qkv(K, 0, 1)
            qkv(K, 0, 2)
            pe.wait_ge(patches_loaded, 32)
            for t in range(IMAGE_TILES):
                what = ("embed", t)
                bank = claim(what)
                matmuls(bank[:, 0:DIM], [(patches[:, f, P * t:P * (t + 1)], w_embed[:, f, :])
                                         for f in range(PATCH_CHUNKS)]).then_inc(bank_full[BANK[what]], 1)
            pe.wait_ge(xn_ready, TILES)
            for k in range(DIM_CHUNKS):
                transpose_xn("xnT", k, 0)
            pe.wait_ge(xT_lo_ready, 2 * GROUPS)
            qkv(V, 0, 0)
            qkv(V, 1, 0)
            qkv(K, 0, 0)
            bank = claim(("absmean",))
            pe.wait_ge(pool_constants, 2)
            pe.wait_ge(abs_ready, 2)
            pe.matmul(bank[:, 0:2], ones[:, :], abs_sums[:, :], start=True, stop=True)\
                .then_inc(bank_full[BANK[("absmean",)]], 1)
            qkv(K, 1, 1)
            qkv(K, 1, 2)
            for group in order:
                value_transpose(0, group)
            qkv(K, 1, 0)
            for group in order:
                value_transpose(1, group)
            for half in range(2):
                gram_product(0, half)
            pe.wait_ge(w_qkv_lo_ready, 3)
            for group in order:
                qkv(Q, 0, group)
            for half in range(2):
                gram_product(1, half)
            for group in order:
                qkv(Q, 1, group)
            bank = claim(("ffn_rows",))
            pe.wait_ge(row_weight_ready, 1)
            pe.wait_ge(down_ready, 4)
            for r in range(2):
                pairs = []
                for c in range(HIDDEN_CHUNKS):
                    col = HIDDEN_CHUNKS * r + c
                    for part in (row_weights_hi, row_weights_lo):
                        pairs.append((part[:, col:col + 1].broadcast_to([P, P]), down_sign[:, DIM * c:DIM * (c + 1)]))
                last = matmuls(bank[:, DIM * r:DIM * (r + 1)], pairs)
            last.then_inc(bank_full[BANK[("ffn_rows",)]], 1)
            pe.wait_ge(gram_ready, 2)
            for group in order:
                mix(0, group)
            pe.wait_ge(gram_ready, 4)
            for group in order:
                mix(1, group)

            def proj_group(s):
                pe.wait_ge(w_proj_lo_ready, 1)
                pe.wait_ge(att_lo_ready, GROUPS + s + 1)
                for pair in range(2):
                    proj(s, pair)

            def x2T_group(s):
                pe.wait_ge(xn_ready, TILES + GROUP_TILES * (s + 1))
                for k in range(DIM_CHUNKS):
                    transpose_xn("x2T", k, order[s])

            proj_group(0)
            proj_group(1)
            x2T_group(0)
            pe.wait_ge(up_ready, 1)
            pe.wait_ge(xT_lo_ready, 2 * GROUPS + 2)
            for i in range(GROUP_TILES):
                up(GROUP_TILES * order[0] + i)
            proj_group(2)
            x2T_group(1)
            for s in range(1, GROUPS):
                pe.wait_ge(xT_lo_ready, 2 * GROUPS + 2 * (s + 1))
                pe.wait_ge(g_ready, GROUP_TILES * s)
                for i in range(GROUP_TILES):
                    gT(s - 1, 2 * i)
                    gT(s - 1, 2 * i + 1)
                    up(GROUP_TILES * order[s] + i)
                if s + 1 < GROUPS:
                    x2T_group(s + 1)
                pe.wait_ge(gT_lo_ready, HIDDEN_CHUNKS * s)
                for i in range(GROUP_TILES):
                    down(s - 1, i)
            pe.wait_ge(g_ready, TILES)
            last_down = [("down", GROUP_TILES * order[-1] + i) for i in range(GROUP_TILES)]
            for c in range(HIDDEN_CHUNKS + 1):
                if c < HIDDEN_CHUNKS:
                    gT(GROUPS - 1, c)
                if c == 0:
                    continue
                pe.wait_ge(gT_lo_ready, HIDDEN_CHUNKS * (GROUPS - 1) + c)
                for i, what in enumerate(last_down):
                    if c == 1:
                        claim(what)
                    for j, (stationary, moving) in enumerate(down_pairs(i, c - 1)):
                        last = pe.matmul(psum[:, BANK[what], 0:DIM], stationary, moving,
                                         start=(c == 1 and j == 0), stop=(c == HIDDEN_CHUNKS and j == 1))
                    if c == HIDDEN_CHUNKS:
                        last.then_inc(bank_full[BANK[what]], 1)

        @blk.scalar
        def _(act):
            def full(what):
                act.wait_ge(bank_full[BANK[what]], nth[what])
                return psum[:, BANK[what], :]

            def w_hi(m):
                e = slice(DIM * m, DIM * (m + 1))
                act.activation(w_qkv_hi[:, :, e], w_qkv[:, :, e], ACT.Copy).then_inc(w_qkv_hi_ready, 1)

            def xT_hi(kind, dst, k, group):
                act.activation(dst[:, k, cols(group)], full((kind, k, group)), ACT.Copy).then_inc(xT_hi_ready, 1)

            def sigmoids(m, c):
                j = qkv_index(m, c)
                act.wait_ge(bn_ready, j + 1)
                for group in order:
                    what = ("qkv", m, c, group)
                    act.activation(act_qkv[:, j, cols(group)], psum[:, BANK[what], :], ACT.Sigmoid,
                                   bias=bn_shift[:, j:j + 1], scale=bn_slope[:, j:j + 1])\
                        .then_inc(sigmoid_ready, 1)

            def values(c, group):
                bank = full(("valueT", c, group))
                which = BANK[("valueT", c, group)]
                if group:
                    act.activation(v_text[:, c, 4 * (group - 1):4 * group, :], bank, ACT.Copy)\
                        .then_inc(value_ready, 1)
                else:
                    act.activation(v_image[:, c, 0, :, :], bank, ACT.Identity, scale=half_mask[0])
                    act.activation(v_image[:, c, 1, :, :], bank, ACT.Identity, scale=half_mask[1])\
                        .then_inc(value_ready, 1)

            def att_hi(c, group):
                act.activation(attT_hi[:, c, cols(group)], full(("mix", c, group)), ACT.Copy).then_inc(att_hi_ready, 1)

            def gelu(s, i):
                t = GROUP_TILES * order[s] + i
                first = full(("up", t))
                full(("up2", t))
                bank = BANK[("up", t)]
                if s >= 2:
                    act.wait_ge(gT_lo_ready, HIDDEN_CHUNKS * (s - 1))
                    act.wait_ge(g_moment, GROUP_TILES * (s - 1))
                act.activation(g[:, GROUP_TILES * (s % 2) + i, :], psum[:, bank:bank + 2, :], ACT.Gelu)\
                    .then_inc(g_ready, 1)

            def g_hi(s, c):
                act.activation(gT_hi[:, c, :], full(("gT", c, order[s])), ACT.Copy, scale=ln_w[:, c:c + 1])\
                    .then_inc(gT_hi_ready, 1)

            act.wait_ge(w_qkv_loaded, 16)
            w_hi(V)
            w_hi(K)
            for group in (1, 2):
                for k in range(DIM_CHUNKS):
                    xT_hi("xnT", xnT_hi, k, group)
            w_hi(Q)
            act.wait_ge(constants_loaded, 48)
            act.activation(row_weights_hi[:, :], columns[:, 12:28], ACT.Copy).then_inc(row_weight_hi_ready, 1)
            for t in range(IMAGE_TILES):
                bank = full(("embed", t))
                act.activation(h[:, t, :], bank[:, 0:DIM], ACT.Copy)\
                    .then_inc(embed_ready, 1)
            act.wait_ge(w_up_loaded, 16)
            act.activation(up_sign[:, :], w_up[:, :], ACT.Abs, accum_out=abs_sums[:, 0:1]).then_inc(abs_ready, 1)
            for k in range(DIM_CHUNKS):
                xT_hi("xnT", xnT_hi, k, 0)
            act.wait_ge(w_down_loaded, 16)
            act.activation(down_sign[:, :], w_down[:, :], ACT.Abs, accum_out=abs_sums[:, 1:2]).then_inc(abs_ready, 1)
            sigmoids(V, 0)
            sigmoids(V, 1)
            for group in order:
                values(0, group)
            sigmoids(K, 0)
            for group in order:
                values(1, group)
            act.wait_ge(w_proj_loaded, 16)
            act.activation(w_proj_hi[:, :, :], w_proj[:, :, :], ACT.Copy).then_inc(w_proj_hi_ready, 1)
            sigmoids(K, 1)
            sigmoids(Q, 0)
            sigmoids(Q, 1)
            for c in range(DIM_CHUNKS):
                for group in order:
                    att_hi(c, group)
            for k in range(DIM_CHUNKS):
                xT_hi("x2T", x2T_hi, k, order[0])
            for i in range(GROUP_TILES):
                gelu(0, i)
            for k in range(DIM_CHUNKS):
                xT_hi("x2T", x2T_hi, k, order[1])
            for s in range(1, GROUPS):
                for i in range(GROUP_TILES):
                    g_hi(s - 1, 2 * i)
                    g_hi(s - 1, 2 * i + 1)
                    gelu(s, i)
                if s + 1 < GROUPS:
                    for k in range(DIM_CHUNKS):
                        xT_hi("x2T", x2T_hi, k, order[s + 1])
            for c in range(HIDDEN_CHUNKS):
                g_hi(GROUPS - 1, c)

        @blk.gpsimd
        def _(pool):
            pool.memset(minus_half[:, :], -0.5).then_inc(pool_constants, 1)
            pool.memset(ones[:, :], 1.0).then_inc(pool_constants, 1)
            pool.wait_ge(pool_constants, 2)

            def norm_rsqrt(layer, n, group):
                pool.wait_ge(norm_var_ready, n)
                ts = slice(GROUP_TILES * group, GROUP_TILES * (group + 1))
                pool.tensor_tensor(norm_rstd[:, layer, ts], norm_var[:, layer, ts], minus_half[:, :], ALU.pow)\
                    .then_inc(norm_rstd_ready, 1)

            def bn_rsqrt(j):
                pool.wait_ge(bn_var_ready, j + 1)
                pool.tensor_tensor(bn_rstd[:, j:j + 1], bn_var[:, j:j + 1], minus_half[:, 0:1], ALU.pow)\
                    .then_inc(bn_rstd_ready, 1)

            def add_bias(n, group):
                pool.wait_ge(xn_ready, GROUP_TILES * (n + 1))
                for t in tiles_of(group):
                    pool.tensor_tensor(h[:, t, :], h[:, t, :], proj_bias[:, :], ALU.add).then_inc(biased, 1)

            def g_rsqrt(s):
                ts = slice(GROUP_TILES * order[s], GROUP_TILES * (order[s] + 1))
                pool.wait_ge(g_var_ready, s + 1)
                pool.tensor_tensor(g_rstd[:, ts], g_var[:, ts], minus_half[:, :], ALU.pow).then_inc(g_rstd_ready, 1)

            def shift_h2(s):
                pool.wait_ge(xn_ready, TILES + GROUP_TILES * (s + 1))
                pool.wait_ge(rows_ready, 1)
                for t in tiles_of(order[s]):
                    pool.tensor_tensor(h[:, t, :], h[:, t, :], rows[:, 1, :], ALU.add).then_inc(h2_shifted, 1)

            norm_rsqrt(0, 1, 1)
            norm_rsqrt(0, 2, 2)
            pool.wait_ge(constants_loaded, 48)
            add_bias(0, 1)
            norm_rsqrt(0, 3, 0)
            bn_rsqrt(0)
            bn_rsqrt(1)
            bn_rsqrt(2)
            bn_rsqrt(3)
            pool.wait_ge(threshold_ready, 2)
            for i in range(4):
                part = slice(512 * i, 512 * (i + 1))
                if i:
                    pool.wait_ge(down_ready, i)
                pool.tensor_scalar(positive[:, :], w_down[:, part], thresholds[:, 0, 1:2], None, ALU.is_gt)\
                    .then_inc(down_part, 1)
                if i == 1:
                    bn_rsqrt(4)
                pool.tensor_scalar(negative[:, :], w_down[:, part], thresholds[:, 1, 1:2], None, ALU.is_lt)\
                    .then_inc(down_part, 1)
                pool.wait_ge(down_part, 2 * i + 2)
                pool.tensor_tensor(down_sign[:, part], positive[:, :], negative[:, :], ALU.subtract)\
                    .then_inc(down_ready, 1)
            for n, group in enumerate(order):
                pool.wait_ge(sigmoid_ready, GROUPS * qkv_index(Q, 0) + n + 1)
                q = act_qkv[:, qkv_index(Q, 0), cols(group)]
                pool.tensor_tensor(q, q, act_qkv[:, qkv_index(K, 0), cols(group)], ALU.mult).then_inc(qk0_ready, 1)
            bn_rsqrt(5)
            add_bias(1, 2)
            add_bias(2, 0)
            for s in range(GROUPS):
                norm_rsqrt(1, GROUPS + s + 1, order[s])
                if s:
                    g_rsqrt(s - 1)
                shift_h2(s)
            g_rsqrt(GROUPS - 1)

        @blk.vector
        def _(dve):
            def full(what):
                dve.wait_ge(bank_full[BANK[what]], nth[what])
                return psum[:, BANK[what], :]

            def norm_statistics(layer, n, group):
                for i, t in enumerate(tiles_of(group)):
                    dve.bn_stats(norm_stats[:, layer, t, :], h[:, t, :]).then_inc(norm_stat, 1)
                for i, t in enumerate(tiles_of(group)):
                    dve.wait_ge(norm_stat, GROUP_TILES * n + i + 1)
                    dve.bn_aggr(norm_moments[:, layer, t, :], norm_stats[:, layer, t, :]).then_inc(norm_moment, 1)
                dve.wait_ge(norm_moment, GROUP_TILES * (n + 1))
                ts = slice(GROUP_TILES * group, GROUP_TILES * (group + 1))
                dve.tensor_scalar(norm_var[:, layer, ts], norm_moments[:, layer, ts, 1], NORM_EPS, None, ALU.add)\
                    .then_inc(norm_var_ready, 1)

            def normalise(layer, n, group):
                dve.wait_ge(norm_rstd_ready, n + 1)
                for t in tiles_of(group):
                    dve.tensor_scalar(xn[:, t, :], h[:, t, :], norm_moments[:, layer, t, 0:1],
                                      norm_rstd[:, layer, t:t + 1], ALU.subtract, ALU.mult).then_inc(xn_ready, 1)

            def w_lo(m):
                e = slice(DIM * m, DIM * (m + 1))
                dve.wait_ge(w_qkv_hi_ready, m + 1)
                dve.tensor_tensor(w_qkv_lo[:, :, e], w_qkv[:, :, e], w_qkv_hi[:, :, e].bitcast(fp32), ALU.subtract)\
                    .then_inc(w_qkv_lo_ready, 1)

            def xT_lo(kind, hi, lo, n, k, group):
                dve.wait_ge(xT_hi_ready, n + 1)
                dve.tensor_tensor(lo[:, k, cols(group)], psum[:, BANK[(kind, k, group)], :],
                                  hi[:, k, cols(group)].bitcast(fp32), ALU.subtract)\
                    .then_inc(xT_lo_ready, 1)

            qkv_stats = []

            def qkv_statistics(m, c, group):
                j = qkv_index(m, c)
                dve.bn_stats(bn_stats[:, j, 6 * group:6 * (group + 1)], full(("qkv", m, c, group)))\
                    .then_inc(bn_stat, 1)
                qkv_stats.append((m, c, group))

            def qkv_affine(m, c):
                j = qkv_index(m, c)
                dve.wait_ge(bn_stat, len(qkv_stats))
                dve.bn_aggr(bn_moments[:, j, :], bn_stats[:, j, :]).then_inc(bn_moment, 1)
                dve.wait_ge(bn_moment, j + 1)
                dve.tensor_scalar(bn_var[:, j:j + 1], bn_moments[:, j, 1:2], NORM_EPS, None, ALU.add)\
                    .then_inc(bn_var_ready, 1)

            def qkv_affine_end(m, c):
                j = qkv_index(m, c)
                dve.wait_ge(bn_rstd_ready, j + 1)
                dve.tensor_tensor(bn_slope[:, j:j + 1], bn_rstd[:, j:j + 1], bn_gain[:, j:j + 1], ALU.mult)\
                    .then_inc(bn_slopes, 1)
                dve.tensor_tensor(bn_minus_slope[:, j:j + 1], bn_rstd[:, j:j + 1], bn_minus_gain[:, j:j + 1], ALU.mult)\
                    .then_inc(bn_slopes, 1)
                dve.wait_ge(bn_slopes, 2 * (j + 1))
                dve.scalar_tensor_tensor(bn_shift[:, j:j + 1], bn_moments[:, j, 0:1], bn_minus_slope[:, j:j + 1],
                                         bn_offset[:, j:j + 1], ALU.mult, ALU.add).then_inc(bn_ready, 1)

            def gram_scaled(c, half):
                what = ("gram", c, half)
                bank = full(what).rearrange("p (b e) -> p b e", b=4)
                mask = head_mask.rearrange("p (a e) -> p a e", a=1).broadcast_to([P, 4, P])
                dve.tensor_tensor(gram[:, c, 4 * half:4 * (half + 1), :], bank, mask, ALU.mult)\
                    .then_inc(gram_ready, 1)

            def att_lo(n, c, group):
                dve.wait_ge(att_hi_ready, n + 1)
                dve.tensor_tensor(attT_lo[:, c, cols(group)], psum[:, BANK[("mix", c, group)], :],
                                  attT_hi[:, c, cols(group)].bitcast(fp32), ALU.subtract)\
                    .then_inc(att_lo_ready, 1)

            def residual(s):
                for pair in range(2):
                    t0 = GROUP_TILES * order[s] + 2 * pair
                    what = ("proj", t0)
                    bank = full(what).rearrange("p (t d) -> p t d", t=2)
                    dve.tensor_tensor(h[:, t0:t0 + 2, :], bank, h[:, t0:t0 + 2, :], ALU.add)\
                        .then_inc(h2_ready, 1)
                dve.wait_ge(h2_ready, 2 * (s + 1))

            def second_norm(s):
                residual(s)
                norm_statistics(1, GROUPS + s, order[s])

            def x2T_lo(s):
                for k in range(DIM_CHUNKS):
                    xT_lo("x2T", x2T_hi, x2T_low, DIM_CHUNKS * (GROUPS + s) + k, k, order[s])

            def g_statistics(s, i):
                t = GROUP_TILES * order[s] + i
                n = GROUP_TILES * s + i
                dve.wait_ge(g_ready, n + 1)
                for half in range(2):
                    dve.bn_stats(g_stats[:, t, half, :], g[:, GROUP_TILES * (s % 2) + i, 512 * half:512 * (half + 1)])\
                        .then_inc(g_stat, 1)
                dve.wait_ge(g_stat, 2 * (n + 1))
                dve.bn_aggr(g_moments[:, t, :], g_stats[:, t, :, :].rearrange("p a b -> p (a b)")).then_inc(g_moment, 1)
                if i == GROUP_TILES - 1:
                    dve.wait_ge(g_moment, n + 1)
                    ts = slice(GROUP_TILES * order[s], GROUP_TILES * (order[s] + 1))
                    dve.tensor_scalar(g_var[:, ts], g_moments[:, ts, 1], NORM_EPS, None, ALU.add).then_inc(g_var_ready, 1)
                    dve.tensor_scalar(g_minus_mean[:, ts], g_moments[:, ts, 0], -1.0, None, ALU.mult)\
                        .then_inc(g_mean_ready, 1)

            def g_lo(s, c):
                dve.wait_ge(gT_hi_ready, HIDDEN_CHUNKS * s + c + 1)
                what = ("gT", c, order[s])
                dve.scalar_tensor_tensor(gT_lo[:, c, :], psum[:, BANK[what], :], ln_w[:, c:c + 1],
                                         gT_hi[:, c, :].bitcast(fp32), ALU.mult, ALU.subtract)\
                    .then_inc(gT_lo_ready, 1)

            def finish(s, i):
                t = GROUP_TILES * order[s] + i
                n = GROUP_TILES * s + i
                what = ("down", t)
                bank = full(what)
                if i == 0:
                    dve.wait_ge(g_rstd_ready, s + 1)
                    dve.wait_ge(g_mean_ready, s + 1)
                    dve.wait_ge(h2_shifted, GROUP_TILES * (s + 1))
                if n >= 2:
                    dve.wait_ge(final_ready, n - 1)
                dve.scalar_tensor_tensor(final[:, n % 2, :], rows[:, 0, :], g_minus_mean[:, t:t + 1], bank[:, 0:DIM],
                                         ALU.mult, ALU.add).then_inc(final_part, 1)
                dve.wait_ge(final_part, n + 1)
                dve.scalar_tensor_tensor(h[:, t, :], final[:, n % 2, :], g_rstd[:, t:t + 1], h[:, t, :],
                                         ALU.mult, ALU.add).then_inc(final_ready, 1)

            dve.wait_ge(text_loaded[0], 16)
            norm_statistics(0, 0, 1)
            dve.wait_ge(text_loaded[1], 16)
            norm_statistics(0, 1, 2)
            normalise(0, 0, 1)
            w_lo(V)
            normalise(0, 1, 2)
            w_lo(K)
            for n, (group, k) in enumerate([(1, 0), (1, 1), (2, 0), (2, 1)]):
                xT_lo("xnT", xnT_hi, xnT_lo, n, k, group)
            dve.wait_ge(constants_loaded, 48)
            dve.tensor_scalar(bn_gain[:, :], gain4, SIGMOID_SLOPE, None, ALU.mult).then_inc(bn_constants, 1)
            dve.tensor_scalar(bn_minus_gain[:, :], gain4, -SIGMOID_SLOPE, None, ALU.mult).then_inc(bn_constants, 1)
            dve.tensor_scalar(bn_offset[:, :], shift, V_THRESHOLD, SIGMOID_SLOPE, ALU.subtract, ALU.mult)\
                .then_inc(bn_constants, 1)
            w_lo(Q)
            dve.wait_ge(row_weight_hi_ready, 1)
            dve.tensor_tensor(row_weights_lo[:, :], columns[:, 12:28], row_weights_hi[:, :].bitcast(fp32),
                              ALU.subtract).then_inc(row_weight_ready, 1)
            for c in range(DIM_CHUNKS):
                for group in (1, 2):
                    qkv_statistics(V, c, group)
            for group in (1, 2):
                qkv_statistics(K, 0, group)
            dve.wait_ge(embed_ready, IMAGE_TILES)
            norm_statistics(0, 2, 0)
            normalise(0, 2, 0)
            for k in range(DIM_CHUNKS):
                xT_lo("xnT", xnT_hi, xnT_lo, 4 + k, k, 0)
            dve.wait_ge(bn_constants, 3)
            qkv_statistics(V, 0, 0)
            qkv_affine(V, 0)
            qkv_statistics(V, 1, 0)
            qkv_affine_end(V, 0)
            qkv_affine(V, 1)
            qkv_statistics(K, 0, 0)
            qkv_affine_end(V, 1)
            qkv_affine(K, 0)
            bank = full(("absmean",))
            dve.tensor_scalar(absmeans[:, :], bank[:, 0:2], 1.0 / (DIM * HIDDEN), ABSMEAN_EPS, ALU.mult, ALU.add)\
                .then_inc(absmean_ready, 1)
            qkv_affine_end(K, 0)
            dve.wait_ge(absmean_ready, 1)
            dve.tensor_scalar(thresholds[:, 0, :], absmeans[:, :], 0.5, None, ALU.mult).then_inc(threshold_ready, 1)
            dve.tensor_scalar(thresholds[:, 1, :], absmeans[:, :], -0.5, None, ALU.mult).then_inc(threshold_ready, 1)
            for group in order:
                qkv_statistics(K, 1, group)
            qkv_affine(K, 1)
            dve.wait_ge(threshold_ready, 2)
            for i in range(4):
                part = slice(512 * i, 512 * (i + 1))
                dve.tensor_scalar(up_negative[:, part], w_up[:, part], thresholds[:, 1, 0:1], None, ALU.is_lt)\
                    .then_inc(up_part, 1)
                if i == 0:
                    qkv_affine_end(K, 1)
            for i in range(2):
                gram_scaled(0, i)
            dve.wait_ge(up_part, 4)
            dve.scalar_tensor_tensor(up_sign[:, :], w_up[:, :], thresholds[:, 0, 0:1], up_negative[:, :],
                                     ALU.is_gt, ALU.subtract).then_inc(up_ready, 1)
            dve.wait_ge(w_proj_hi_ready, 1)
            dve.tensor_tensor(w_proj_lo[:, :, :], w_proj[:, :, :], w_proj_hi[:, :, :].bitcast(fp32), ALU.subtract)\
                .then_inc(w_proj_lo_ready, 1)
            for group in order:
                qkv_statistics(Q, 0, group)
            qkv_affine(Q, 0)
            for i in range(2):
                gram_scaled(1, i)
            qkv_affine_end(Q, 0)
            for group in order:
                qkv_statistics(Q, 1, group)
            qkv_affine(Q, 1)
            qkv_affine_end(Q, 1)
            bank = full(("ffn_rows",))
            dve.tensor_copy(rows[:, :, :], bank.rearrange("p (r d) -> p r d", r=2))\
                .then_inc(rows_ready, 1)
            for n, group in enumerate(order):
                dve.wait_ge(sigmoid_ready, GROUPS * qkv_index(Q, 1) + n + 1)
                q = act_qkv[:, qkv_index(Q, 1), cols(group)]
                dve.tensor_tensor(q, q, act_qkv[:, qkv_index(K, 1), cols(group)], ALU.mult).then_inc(qk1_ready, 1)
            for c in range(DIM_CHUNKS):
                for n, group in enumerate(order):
                    att_lo(GROUPS * c + n, c, group)
            dve.wait_ge(biased, TILES)
            second_norm(0)
            normalise(1, GROUPS, order[0])
            second_norm(1)
            x2T_lo(0)
            normalise(1, GROUPS + 1, order[1])
            dve.wait_ge(rows_ready, 1)
            for i in range(GROUP_TILES):
                g_statistics(0, i)
            second_norm(2)
            x2T_lo(1)
            normalise(1, GROUPS + 2, order[2])
            for s in range(1, GROUPS):
                for i in range(GROUP_TILES):
                    g_lo(s - 1, 2 * i)
                    g_lo(s - 1, 2 * i + 1)
                    g_statistics(s, i)
                if s + 1 < GROUPS:
                    x2T_lo(s + 1)
                for i in range(GROUP_TILES):
                    finish(s - 1, i)
            for c in range(HIDDEN_CHUNKS):
                g_lo(GROUPS - 1, c)
            for i in range(GROUP_TILES):
                finish(GROUPS - 1, i)


_SHAPE = (TILES, P, DIM)


def kernel(**inputs):
    import concourse.bacc as _bacc
    from concourse.bass_utils import run_bass_kernel_spmd as _run

    a = {k: np.asarray(v) for k, v in inputs.items()}

    def feature_major(m, chunks):
        return np.ascontiguousarray(m.reshape(chunks, P, -1).transpose(1, 0, 2))

    side = a["x"].shape[1] // PATCH
    image = a["x"].reshape(BATCHES, side, PATCH, side, PATCH, 3).transpose(2, 4, 5, 0, 1, 3)
    image = image.reshape(PATCH_FEATURES, BATCHES * IMAGE_TOKENS)
    w_qkv = np.concatenate([a["L0_attn_Wv"].T, a["L0_attn_Wk"].T, a["L0_attn_Wq"].T], axis=1)
    halves = np.zeros((P, 2), np.float32)
    halves[:64, 0] = 1.0
    halves[64:, 1] = 1.0
    columns = np.concatenate(
        [a[f"L0_attn_{n}{m}"].reshape(2, P).T for n in "gb" for m in "vkq"]
        + [a["L0_ffn_ln_w"].reshape(8, P).T, a["L0_ffn_ln_b"].reshape(8, P).T, halves], axis=1)
    head = np.arange(P) // HEAD_DIM
    squares = np.concatenate(
        [np.eye(P, dtype=np.float32),
         np.where(head[:, None] == head[None, :], np.float32(HEAD_DIM ** -0.5), np.float32(0))], axis=1)
    arrays = {
        "patches_in": feature_major(image, PATCH_CHUNKS),
        "text_in": np.ascontiguousarray(a["txt"].transpose(1, 0, 2)),
        "w_embed_in": feature_major(a["L0_tok_W"], PATCH_CHUNKS),
        "w_qkv_in": feature_major(w_qkv, DIM_CHUNKS),
        "w_proj_in": feature_major(a["L0_attn_Wp"].T, DIM_CHUNKS),
        "w_up_in": feature_major(a["L0_ffn_W_fc"].T, DIM_CHUNKS).reshape(P, -1),
        "w_down_in": feature_major(a["L0_ffn_W_proj"].T, HIDDEN_CHUNKS).reshape(P, -1),
        "columns_in": np.ascontiguousarray(columns),
        "proj_bias_in": a["L0_attn_bp"],
        "squares_in": np.ascontiguousarray(squares),
    }
    nc = _bacc.Bacc("TRN2", target_bir_lowering=False, num_devices=1)
    args = {n: nc.dram_tensor(n, v.shape, mybir.dt.from_np(v.dtype), kind="ExternalInput").ap()
            for n, v in arrays.items()}
    out = nc.dram_tensor("out", _SHAPE, mybir.dt.float32, kind="ExternalOutput").ap()
    block(nc, *args.values(), out)
    r = _run(nc, [arrays], core_ids=[0]).results[0]["out"]
    result = np.empty((BATCHES, IMAGE_TOKENS + TEXT_TOKENS, DIM), r.dtype)
    result[:, :IMAGE_TOKENS] = r[:IMAGE_TILES].reshape(BATCHES, IMAGE_TOKENS, DIM)
    result[:, IMAGE_TOKENS:] = r[IMAGE_TILES:]
    return result
```

```python
import numpy as np
import concourse.bass as bass
from concourse import mybir
from contextlib import ExitStack

P = 128
BATCHES, IMAGE_TOKENS, TEXT_TOKENS = 8, 64, 128
DIM, HEADS, HIDDEN = 256, 16, 1024
HEAD_DIM = DIM // HEADS
PATCH = 16
PATCH_FEATURES = 3 * PATCH * PATCH
TOKENS = BATCHES * (IMAGE_TOKENS + TEXT_TOKENS)
TILES = TOKENS // P
IMAGE_TILES = BATCHES * IMAGE_TOKENS // P
GROUP_TILES = 4
GROUP = GROUP_TILES * P
GROUPS = TILES // GROUP_TILES
DIM_CHUNKS = DIM // P
HIDDEN_CHUNKS = HIDDEN // P
PATCH_CHUNKS = PATCH_FEATURES // P
NORM_EPS = 1e-5
ABSMEAN_EPS = 1e-6
V_THRESHOLD, SIGMOID_SLOPE = 1.0, 4.0
V, K, Q = 0, 1, 2

GROUP_ORDER = (1, 2, 0)


def bank_uses():
    uses = []
    first, second, image = GROUP_ORDER

    def use(what, bank):
        uses.append((what, bank))

    def use_groups(kind, index, banks):
        for group, bank in zip(GROUP_ORDER, banks):
            use((kind, *index, group), bank)

    for t in range(IMAGE_TILES):
        use(("embed", t), t)
    for n, group in enumerate((first, second)):
        for k in range(DIM_CHUNKS):
            use(("xnT", k, group), 4 + 2 * n + k)
    for c in range(DIM_CHUNKS):
        for n, group in enumerate((first, second)):
            use(("qkv", V, c, group), 2 * c + n)
    for k in range(DIM_CHUNKS):
        use(("xnT", k, image), 4 + k)
    for c in range(DIM_CHUNKS):
        use(("qkv", V, c, image), 6 + c)
    use_groups("qkv", (K, 0), (4, 5, 0))
    use_groups("qkv", (K, 1), (1, 6, 2))
    use(("absmean",), 3)
    use_groups("valueT", (0,), (3, 7, 3))
    use_groups("qkv", (Q, 0), (4, 5, 0))
    use_groups("qkv", (Q, 1), (1, 6, 2))
    use_groups("valueT", (1,), (7, 3, 7))
    for c in range(DIM_CHUNKS):
        for half in range(2):
            use(("gram", c, half), (3, 7)[half])
    use(("mix", 0, first), 4)
    use(("mix", 1, first), 5)
    use(("mix", 0, second), 0)
    use(("mix", 1, second), 1)

    def proj(group):
        for pair in range(2):
            use(("proj", GROUP_TILES * group + 2 * pair), 6 + pair)

    def x2T(group):
        for k in range(DIM_CHUNKS):
            use(("x2T", k, group), 4 + k)

    proj(first)
    use(("mix", 0, image), 3)
    use(("mix", 1, image), 2)
    proj(second)
    use(("ffn_rows",), 0)
    proj(image)
    x2T(first)
    for i in range(GROUP_TILES):
        use(("up", GROUP_TILES * first + i), 2 * (i % 2))
    x2T(second)
    for before, group, after in ((first, second, image), (second, image, None)):
        for i in range(GROUP_TILES):
            for c in (2 * i, 2 * i + 1):
                use(("gT", c, before), 4 + c % 2)
            use(("up", GROUP_TILES * group + i), 2 * (i % 2))
        if after is not None:
            x2T(after)
        for i in range(GROUP_TILES):
            use(("down", GROUP_TILES * before + i), 6 + i % 2)
    for c in range(HIDDEN_CHUNKS):
        use(("gT", c, image), 4 + c % 4)
    for i in range(GROUP_TILES):
        use(("down", GROUP_TILES * image + i), i)
    return uses


def block(
    nc, embed_in, text_in, w_qkv_in, w_proj_in, w_up_in, w_down_in,
    columns_in, proj_bias_in, squares_in, out,
):
    fp32, fp32r = mybir.dt.float32, mybir.dt.float32r
    ALU, ACT = mybir.AluOpType, mybir.ActivationFunctionType

    with ExitStack() as ctx:
        def sem(name):
            return ctx.enter_context(nc.semaphore(name))

        offset = [nc.sbuf_base]
        floats = 4

        def place(name, shape, dt=fp32, at=None):
            size = int(np.prod(shape[1:])) * floats
            if at is None:
                at = -(-offset[0] // 32) * 32
                offset[0] = at + size
            return nc.alloc_sbuf_tensor_at(name, shape, dt, offset=at), at, at + size

        h, _, _ = place("h", [P, TILES, DIM])
        xn, _, _ = place("xn", [P, TILES, DIM])
        xnT_hi, at_xnT, _ = place("xnT_hi", [P, DIM_CHUNKS, TOKENS], fp32r)
        xnT_lo, at_xnT_lo, _ = place("xnT_lo", [P, DIM_CHUNKS, TOKENS], fp32r)
        attT_hi, _, _ = place("attT_hi", [P, DIM_CHUNKS, TOKENS], fp32r, at_xnT)
        attT_lo, _, _ = place("attT_lo", [P, DIM_CHUNKS, TOKENS], fp32r, at_xnT_lo)
        x2T_hi, at_x2T, _ = place("x2T_hi", [P, DIM_CHUNKS, TOKENS], fp32r)
        x2T_low, _, _ = place("x2T_low", [P, DIM_CHUNKS, TOKENS], fp32r)
        embed, _, _ = place("embed", [P, PATCH_CHUNKS, GROUP + DIM], fp32, at_x2T)
        act_qkv, at_qkv, _ = place("act_qkv", [P, 3 * DIM_CHUNKS, TOKENS])
        gT_hi, _, after = place("gT_hi", [P, HIDDEN_CHUNKS, GROUP], fp32r, at_qkv)
        gT_lo, _, _ = place("gT_lo", [P, HIDDEN_CHUNKS, GROUP], fp32r, after)
        g, at_g, _ = place("g", [P, 2 * GROUP_TILES, HIDDEN])
        v_text, _, after = place("v_text", [P, DIM_CHUNKS, BATCHES, P], fp32, at_g)
        v_image, _, after = place("v_image", [P, DIM_CHUNKS, 2, IMAGE_TILES, P], fp32, after)
        gram, _, after = place("gram", [P, DIM_CHUNKS, BATCHES, P], fp32, after)
        w_qkv, _, after = place("w_qkv", [P, DIM_CHUNKS, 3 * DIM], fp32, after)
        w_proj, _, _ = place("w_proj", [P, DIM_CHUNKS, DIM], fp32, after)
        w_qkv_hi, _, _ = place("w_qkv_hi", [P, DIM_CHUNKS, 3 * DIM], fp32r)
        w_qkv_lo, _, _ = place("w_qkv_lo", [P, DIM_CHUNKS, 3 * DIM], fp32r)
        w_proj_hi, _, _ = place("w_proj_hi", [P, DIM_CHUNKS, DIM], fp32r)
        w_proj_lo, _, _ = place("w_proj_lo", [P, DIM_CHUNKS, DIM], fp32r)
        w_up, _, _ = place("w_up", [P, DIM_CHUNKS * HIDDEN])
        w_down, _, _ = place("w_down", [P, HIDDEN_CHUNKS * DIM])
        up_sign, _, _ = place("up_sign", [P, DIM_CHUNKS * HIDDEN], fp32r)
        down_sign, _, _ = place("down_sign", [P, HIDDEN_CHUNKS * DIM], fp32r)
        up_negative, _, after = place("up_negative", [P, DIM_CHUNKS * HIDDEN], fp32, at_x2T)
        negative, _, after = place("negative", [P, 512], fp32, after)
        positive, _, _ = place("positive", [P, 512], fp32, after)
        squares, _, _ = place("squares", [P, 2 * P])
        columns, _, _ = place("columns", [P, 30])
        proj_bias, _, _ = place("proj_bias", [P, DIM])
        ones, _, _ = place("ones", [P, P])
        minus_half, _, _ = place("minus_half", [P, GROUP_TILES])
        rows, _, _ = place("rows", [P, 2, DIM])
        row_weights_hi, _, _ = place("row_weights_hi", [P, 2 * HIDDEN_CHUNKS], fp32r)
        row_weights_lo, _, _ = place("row_weights_lo", [P, 2 * HIDDEN_CHUNKS], fp32r)
        norm_stats, _, _ = place("norm_stats", [P, 2, TILES, 6])
        norm_moments, _, _ = place("norm_moments", [P, 2, TILES, 2])
        norm_var, _, _ = place("norm_var", [P, 2, TILES])
        norm_rstd, _, _ = place("norm_rstd", [P, 2, TILES])
        bn_stats, _, _ = place("bn_stats", [P, 3 * DIM_CHUNKS, GROUPS * 6])
        bn_moments, _, _ = place("bn_moments", [P, 3 * DIM_CHUNKS, 2])
        bn_var, _, _ = place("bn_var", [P, 3 * DIM_CHUNKS])
        bn_rstd, _, _ = place("bn_rstd", [P, 3 * DIM_CHUNKS])
        bn_slope, _, _ = place("bn_slope", [P, 3 * DIM_CHUNKS])
        bn_minus_slope, _, _ = place("bn_minus_slope", [P, 3 * DIM_CHUNKS])
        bn_shift, _, _ = place("bn_shift", [P, 3 * DIM_CHUNKS])
        g_stats, _, _ = place("g_stats", [P, TILES, 2, 6])
        g_moments, _, _ = place("g_moments", [P, TILES, 2])
        g_var, _, _ = place("g_var", [P, TILES])
        g_rstd, _, _ = place("g_rstd", [P, TILES])
        g_minus_mean, _, _ = place("g_minus_mean", [P, TILES])
        g_mean_slope, _, _ = place("g_mean_slope", [P, TILES])
        g_sum, _, _ = place("g_sum", [P, TILES])
        g_square, _, _ = place("g_square", [P, TILES])
        square_scratch, _, _ = place("square_scratch", [P, HIDDEN], mybir.dt.bfloat16)
        abs_sums, _, _ = place("abs_sums", [P, 2])
        absmeans, _, _ = place("absmeans", [P, 2])
        thresholds, _, _ = place("thresholds", [P, 2, 2])
        row_term, _, _ = place("row_term", [P, DIM])

        identity, head_mask = squares[:, 0:P], squares[:, P:2 * P]
        gain4 = columns[:, 0:6]
        shift = columns[:, 6:12]
        ln_w, ln_b = columns[:, 12:20], columns[:, 20:28]
        half_mask = (columns[:, 28:29], columns[:, 29:30])
        bn_gain, _, _ = place("bn_gain", [P, 6])
        bn_minus_gain, _, _ = place("bn_minus_gain", [P, 6])
        bn_offset, _, _ = place("bn_offset", [P, 6])
        assert offset[0] <= nc.sbuf_usable_end, offset[0]

        psum = ctx.enter_context(nc.psum_tensor("psum", [P, 8, 512], fp32))

        order = GROUP_ORDER

        def tiles_of(group):
            return range(GROUP_TILES * group, GROUP_TILES * (group + 1))

        nth, BANK, BEFORE = {}, {}, {}
        held = [[] for _ in range(8)]

        def hold(what, bank):
            BEFORE[what] = held[bank][-1] if held[bank] else None
            held[bank].append(what)
            nth[what], BANK[what] = len(held[bank]), bank

        for what, bank in bank_uses():
            hold(what, bank)
            if what[0] == "up":
                hold(("up2", what[1]), bank + 1)

        bank_full = [sem(f"bank_full{b}") for b in range(8)]

        text_loaded = [sem("text_loaded_g1"), sem("text_loaded_g2")]
        w_qkv_loaded = sem("w_qkv_loaded")
        constants_loaded = sem("constants_loaded")
        embed_loaded = [sem(f"embed_loaded{f}") for f in range(PATCH_CHUNKS)]
        identity_loaded = sem("identity_loaded")
        w_proj_loaded = sem("w_proj_loaded")
        w_up_loaded = sem("w_up_loaded")
        w_down_loaded = sem("w_down_loaded")
        out_stored = sem("out_stored")
        w_qkv_hi_ready, w_qkv_lo_ready = sem("w_qkv_hi_ready"), sem("w_qkv_lo_ready")
        w_proj_hi_ready, w_proj_lo_ready = sem("w_proj_hi_ready"), sem("w_proj_lo_ready")
        pool_constants = sem("pool_constants")
        norm_stat, norm_moment = sem("norm_stat"), sem("norm_moment")
        norm_var_ready, norm_rstd_ready = sem("norm_var_ready"), sem("norm_rstd_ready")
        xn_ready = sem("xn_ready")
        xT_hi_ready, xT_lo_ready = sem("xT_hi_ready"), sem("xT_lo_ready")
        bn_constants = sem("bn_constants")
        bn_stat, bn_moment = sem("bn_stat"), sem("bn_moment")
        bn_var_ready, bn_rstd_ready = sem("bn_var_ready"), sem("bn_rstd_ready")
        bn_slopes, bn_ready = sem("bn_slopes"), sem("bn_ready")
        sigmoid_ready = sem("sigmoid_ready")
        abs_ready, absmean_ready, threshold_ready = sem("abs_ready"), sem("absmean_ready"), sem("threshold_ready")
        up_part, down_part = sem("up_part"), sem("down_part")
        up_ready, down_ready = sem("up_ready"), sem("down_ready")
        value_ready, gram_ready = sem("value_ready"), sem("gram_ready")
        qk0_ready, qk1_ready = sem("qk0_ready"), sem("qk1_ready")
        att_hi_ready, att_lo_ready = sem("att_hi_ready"), sem("att_lo_ready")
        embed_ready, biased = sem("embed_ready"), sem("biased")
        h2_ready, h2_shifted = sem("h2_ready"), sem("h2_shifted")
        row_weight_hi_ready, row_weight_ready = sem("row_weight_hi_ready"), sem("row_weight_ready")
        rows_ready = sem("rows_ready")
        g_ready = sem("g_ready")
        g_stat, g_moment = sem("g_stat"), sem("g_moment")
        g_var_ready, g_rstd_ready, g_mean_ready = sem("g_var_ready"), sem("g_rstd_ready"), sem("g_mean_ready")
        gT_hi_ready, gT_lo_ready = sem("gT_hi_ready"), sem("gT_lo_ready")
        final_ready = sem("final_ready")
        g_odd_mean, g_odd_square = sem("g_odd_mean"), sem("g_odd_square")
        g_mean_slope_ready, row_term_ready = sem("g_mean_slope_ready"), sem("row_term_ready")
        h2_complete = sem("h2_complete")
        final_order = [GROUP_TILES * gr + i for gr in order for i in range(GROUP_TILES)]

        def place_of(t):
            return GROUP_TILES * order.index(t // GROUP_TILES) + t % GROUP_TILES

        def was_read(what):
            kind, *at = what
            if kind == "xnT":
                k, group = at
                return xT_lo_ready, DIM_CHUNKS * order.index(group) + k + 1
            if kind == "x2T":
                k, group = at
                return xT_lo_ready, DIM_CHUNKS * (GROUPS + order.index(group)) + k + 1
            if kind == "embed":
                return embed_ready, at[0] + 1
            if kind == "qkv":
                m, c, group = at
                return sigmoid_ready, GROUPS * (DIM_CHUNKS * m + c) + order.index(group) + 1
            if kind == "absmean":
                return absmean_ready, 1
            if kind == "valueT":
                c, group = at
                return value_ready, GROUPS * c + order.index(group) + 1
            if kind == "gram":
                c, half = at
                return gram_ready, 2 * c + half + 1
            if kind == "ffn_rows":
                return rows_ready, 1
            if kind == "mix":
                c, group = at
                return att_lo_ready, DIM_CHUNKS * order.index(group) + c + 1
            if kind == "proj":
                return h2_ready, place_of(at[0]) // 2 + 1
            if kind in ("up", "up2"):
                return g_ready, place_of(at[0]) + 1
            if kind == "gT":
                c, group = at
                return gT_lo_ready, HIDDEN_CHUNKS * order.index(group) + c + 1
            return final_ready, place_of(at[0]) + 1

        def cols(group):
            return slice(GROUP * group, GROUP * (group + 1))

        def qkv_index(m, c):
            return DIM_CHUNKS * m + c

        blk = ctx.enter_context(nc.Block())

        @blk.sync
        def _(sp):
            for f in range(PATCH_CHUNKS):
                sp.dma_start(embed[:, f, :], embed_in[:, f, :]).then_inc(embed_loaded[f], 16)
                if f in (1, 3):
                    tiles = slice(GROUP_TILES * (f // 2), GROUP_TILES * (f // 2 + 1))
                    sp.dma_start(h[:, GROUP_TILES * (f // 2 + 1):GROUP_TILES * (f // 2 + 2), :], text_in[:, tiles, :])\
                        .then_inc(text_loaded[f // 2], 16)
                if f == 3:
                    sp.dma_start(squares[:, :], squares_in).then_inc(identity_loaded, 16)
            sp.dma_start(w_qkv[:, :, :], w_qkv_in).then_inc(w_qkv_loaded, 16)
            sp.dma_start(columns[:, :], columns_in).then_inc(constants_loaded, 16)
            sp.dma_start(proj_bias[:, :], proj_bias_in.partition_broadcast(P)).then_inc(constants_loaded, 16)
            sp.dma_start(w_up[:, :], w_up_in).then_inc(w_up_loaded, 16)
            sp.dma_start(w_down[:, :], w_down_in).then_inc(w_down_loaded, 16)
            sp.dma_start(w_proj[:, :, :], w_proj_in).then_inc(w_proj_loaded, 16)
            for n, t in enumerate(final_order):
                sp.wait_ge(final_ready, n + 1)
                sp.dma_start(out[t], h[:, t, :]).then_inc(out_stored, 16)
            sp.wait_ge(out_stored, 16 * TILES)

        @blk.tensor
        def _(pe):
            def claim(what):
                if BEFORE[what]:
                    pe.wait_ge(*was_read(BEFORE[what]))
                return psum[:, BANK[what], :]

            def matmuls(dst, pairs):
                for i, (stationary, moving) in enumerate(pairs):
                    last = pe.matmul(dst, stationary, moving, start=(i == 0), stop=(i == len(pairs) - 1))
                return last

            def transposes(what, sources):
                bank = claim(what)
                for i, source in enumerate(sources):
                    last = pe.transpose(bank[:, P * i:P * (i + 1)], source, identity)
                last.then_inc(bank_full[BANK[what]], 1)

            def transpose_xn(kind, k, group):
                transposes((kind, k, group), [xn[:, t, P * k:P * (k + 1)] for t in tiles_of(group)])

            def qkv(m, c, group):
                what = ("qkv", m, c, group)
                bank = claim(what)
                e = slice(DIM * m + P * c, DIM * m + P * (c + 1))
                pairs = []
                for k in range(DIM_CHUNKS):
                    pairs += [(w_qkv_hi[:, k, e], xnT_hi[:, k, cols(group)]),
                              (w_qkv_hi[:, k, e], xnT_lo[:, k, cols(group)]),
                              (w_qkv_lo[:, k, e], xnT_hi[:, k, cols(group)])]
                matmuls(bank, pairs).then_inc(bank_full[BANK[what]], 1)

            def value_transpose(c, group):
                pe.wait_ge(sigmoid_ready, GROUPS * c + order.index(group) + 1)
                transposes(("valueT", c, group),
                           [act_qkv[:, qkv_index(V, c), P * t:P * (t + 1)] for t in tiles_of(group)])

            def gram_product(c, half):
                what = ("gram", c, half)
                bank = claim(what)
                pe.wait_ge(value_ready, GROUPS * (c + 1))
                for i in range(4):
                    b = 4 * half + i
                    vt, vi = v_text[:, c, b, :], v_image[:, c, b % 2, b // 2, :]
                    last = matmuls(bank[:, P * i:P * (i + 1)], [(vt, vt), (vi, vi)])
                last.then_inc(bank_full[BANK[what]], 1)

            def mix(c, group):
                what = ("mix", c, group)
                bank = claim(what)
                qk = act_qkv[:, qkv_index(Q, c), :]
                if group:
                    batches, width, first = range(4 * (group - 1), 4 * group), TEXT_TOKENS, GROUP * group
                else:
                    batches, width, first = range(BATCHES), IMAGE_TOKENS, 0
                pe.wait_ge((qk0_ready, qk1_ready)[c], order.index(group) + 1)
                for i, b in enumerate(batches):
                    last = pe.matmul(bank[:, width * i:width * (i + 1)], gram[:, c, b, :],
                                     qk[:, first + width * i:first + width * (i + 1)], start=True, stop=True)
                last.then_inc(bank_full[BANK[what]], 1)

            def proj(s, pair):
                t0 = GROUP_TILES * order[s] + 2 * pair
                what = ("proj", t0)
                bank = claim(what)
                for i in range(2):
                    at = slice(P * (t0 + i), P * (t0 + i + 1))
                    pairs = []
                    for c in range(DIM_CHUNKS):
                        pairs += [(attT_hi[:, c, at], w_proj_hi[:, c, :]),
                                  (attT_hi[:, c, at], w_proj_lo[:, c, :]),
                                  (attT_lo[:, c, at], w_proj_hi[:, c, :])]
                    last = matmuls(bank[:, DIM * i:DIM * (i + 1)], pairs)
                last.then_inc(bank_full[BANK[what]], 1)

            def up(t):
                claim(("up", t))
                claim(("up2", t))
                at = slice(P * t, P * (t + 1))
                for half in range(2):
                    pairs = []
                    for k in range(DIM_CHUNKS):
                        w = up_sign[:, HIDDEN * k + 512 * half:HIDDEN * k + 512 * (half + 1)]
                        pairs += [(x2T_hi[:, k, at], w), (x2T_low[:, k, at], w)]
                    matmuls(psum[:, BANK[("up", t)] + half, :], pairs).then_inc(bank_full[BANK[("up", t)] + half], 1)

            def gT(s, c):
                transposes(("gT", c, order[s]),
                           [g[:, GROUP_TILES * (s % 2) + i, P * c:P * (c + 1)] for i in range(GROUP_TILES)])

            def down_pairs(i, c):
                w = down_sign[:, DIM * c:DIM * (c + 1)]
                at = slice(P * i, P * (i + 1))
                return [(gT_hi[:, c, at], w), (gT_lo[:, c, at], w)]

            def down(s, i):
                what = ("down", GROUP_TILES * order[s] + i)
                bank = claim(what)
                matmuls(bank[:, 0:DIM], [p for c in range(HIDDEN_CHUNKS) for p in down_pairs(i, c)])\
                    .then_inc(bank_full[BANK[what]], 1)

            for f in range(PATCH_CHUNKS):
                if f == PATCH_CHUNKS - 1:
                    pe.wait_ge(identity_loaded, 16)
                    for n, group in enumerate((1, 2)):
                        pe.wait_ge(xn_ready, GROUP_TILES * (n + 1))
                        for k in range(DIM_CHUNKS):
                            transpose_xn("xnT", k, group)
                pe.wait_ge(embed_loaded[f], 16)
                for t in range(IMAGE_TILES):
                    last = pe.matmul(psum[:, BANK[("embed", t)], 0:DIM], embed[:, f, P * t:P * (t + 1)],
                                     embed[:, f, GROUP:GROUP + DIM], start=(f == 0), stop=(f == PATCH_CHUNKS - 1))
                    if f == PATCH_CHUNKS - 1:
                        last.then_inc(bank_full[BANK[("embed", t)]], 1)
            pe.wait_ge(w_qkv_lo_ready, 1)
            for c in range(DIM_CHUNKS):
                for n, group in enumerate((1, 2)):
                    pe.wait_ge(xT_lo_ready, 2 * (n + 1))
                    qkv(V, c, group)
            pe.wait_ge(xn_ready, TILES)
            for k in range(DIM_CHUNKS):
                transpose_xn("xnT", k, 0)
            pe.wait_ge(xT_lo_ready, 2 * GROUPS)
            qkv(V, 0, 0)
            qkv(V, 1, 0)
            pe.wait_ge(w_qkv_lo_ready, 2)
            for group in order:
                qkv(K, 0, group)
            for group in order:
                qkv(K, 1, group)
            bank = claim(("absmean",))
            pe.wait_ge(pool_constants, 2)
            pe.wait_ge(abs_ready, 2)
            pe.matmul(bank[:, 0:2], ones[:, :], abs_sums[:, :], start=True, stop=True)\
                .then_inc(bank_full[BANK[("absmean",)]], 1)
            for group in order:
                value_transpose(0, group)
            pe.wait_ge(w_qkv_lo_ready, 3)
            for group in order:
                qkv(Q, 0, group)
            for group in order:
                qkv(Q, 1, group)
            for group in order:
                value_transpose(1, group)
            for c in range(DIM_CHUNKS):
                for half in range(2):
                    gram_product(c, half)

            def proj_group(s):
                pe.wait_ge(w_proj_lo_ready, 1)
                pe.wait_ge(att_lo_ready, DIM_CHUNKS * (s + 1))
                for pair in range(2):
                    proj(s, pair)

            def x2T_group(s):
                pe.wait_ge(xn_ready, TILES + GROUP_TILES * (s + 1))
                for k in range(DIM_CHUNKS):
                    transpose_xn("x2T", k, order[s])

            pe.wait_ge(gram_ready, 4)
            for group in order[:2]:
                for c in range(DIM_CHUNKS):
                    mix(c, group)
            proj_group(0)
            for c in range(DIM_CHUNKS):
                mix(c, order[2])
            proj_group(1)
            bank = claim(("ffn_rows",))
            pe.wait_ge(row_weight_ready, 1)
            pe.wait_ge(down_ready, 4)
            for r in range(2):
                pairs = []
                for c in range(HIDDEN_CHUNKS):
                    col = HIDDEN_CHUNKS * r + c
                    for part in (row_weights_hi, row_weights_lo):
                        pairs.append((part[:, col:col + 1].broadcast_to([P, P]), down_sign[:, DIM * c:DIM * (c + 1)]))
                last = matmuls(bank[:, DIM * r:DIM * (r + 1)], pairs)
            last.then_inc(bank_full[BANK[("ffn_rows",)]], 1)
            proj_group(2)
            x2T_group(0)
            pe.wait_ge(up_ready, 1)
            pe.wait_ge(xT_lo_ready, 2 * GROUPS + 2)
            for i in range(GROUP_TILES):
                up(GROUP_TILES * order[0] + i)
            x2T_group(1)
            for s in range(1, GROUPS):
                pe.wait_ge(g_ready, GROUP_TILES * s)
                for i in range(GROUP_TILES):
                    gT(s - 1, 2 * i)
                    gT(s - 1, 2 * i + 1)
                    if i == 0:
                        pe.wait_ge(xT_lo_ready, 2 * GROUPS + 2 * (s + 1))
                    up(GROUP_TILES * order[s] + i)
                if s + 1 < GROUPS:
                    x2T_group(s + 1)
                pe.wait_ge(gT_lo_ready, HIDDEN_CHUNKS * s)
                for i in range(GROUP_TILES):
                    down(s - 1, i)
            pe.wait_ge(g_ready, TILES)
            last_down = [("down", GROUP_TILES * order[-1] + i) for i in range(GROUP_TILES)]
            AHEAD = 2
            for c in range(-AHEAD, HIDDEN_CHUNKS):
                if c + AHEAD < HIDDEN_CHUNKS:
                    gT(GROUPS - 1, c + AHEAD)
                if c < 0:
                    continue
                pe.wait_ge(gT_lo_ready, HIDDEN_CHUNKS * (GROUPS - 1) + c + 1)
                for i, what in enumerate(last_down):
                    if c == 0:
                        claim(what)
                    for j, (stationary, moving) in enumerate(down_pairs(i, c)):
                        last = pe.matmul(psum[:, BANK[what], 0:DIM], stationary, moving,
                                         start=(c == 0 and j == 0), stop=(c == HIDDEN_CHUNKS - 1 and j == 1))
                    if c == HIDDEN_CHUNKS - 1:
                        last.then_inc(bank_full[BANK[what]], 1)

        @blk.scalar
        def _(act):
            def full(what):
                act.wait_ge(bank_full[BANK[what]], nth[what])
                return psum[:, BANK[what], :]

            def w_hi(m):
                e = slice(DIM * m, DIM * (m + 1))
                act.activation(w_qkv_hi[:, :, e], w_qkv[:, :, e], ACT.Copy).then_inc(w_qkv_hi_ready, 1)

            def xT_hi(kind, dst, k, group):
                act.activation(dst[:, k, cols(group)], full((kind, k, group)), ACT.Copy).then_inc(xT_hi_ready, 1)

            def sigmoids(m, c):
                j = qkv_index(m, c)
                act.wait_ge(bn_ready, j + 1)
                for group in order:
                    what = ("qkv", m, c, group)
                    act.activation(act_qkv[:, j, cols(group)], psum[:, BANK[what], :], ACT.Sigmoid,
                                   bias=bn_shift[:, j:j + 1], scale=bn_slope[:, j:j + 1])\
                        .then_inc(sigmoid_ready, 1)

            def values(c, group):
                bank = full(("valueT", c, group))
                which = BANK[("valueT", c, group)]
                if group:
                    act.activation(v_text[:, c, 4 * (group - 1):4 * group, :], bank, ACT.Copy)\
                        .then_inc(value_ready, 1)
                else:
                    act.activation(v_image[:, c, 0, :, :], bank, ACT.Identity, scale=half_mask[0])
                    act.activation(v_image[:, c, 1, :, :], bank, ACT.Identity, scale=half_mask[1])\
                        .then_inc(value_ready, 1)

            def att_hi(c, group):
                act.activation(attT_hi[:, c, cols(group)], full(("mix", c, group)), ACT.Copy).then_inc(att_hi_ready, 1)

            def gelu(s, i):
                t = GROUP_TILES * order[s] + i
                first = full(("up", t))
                full(("up2", t))
                bank = BANK[("up", t)]
                if s >= 2:
                    act.wait_ge(gT_lo_ready, HIDDEN_CHUNKS * (s - 1))
                    act.wait_ge(g_moment, GROUP_TILES // 2 * (s - 1))
                row = g[:, GROUP_TILES * (s % 2) + i, :]
                if i % 2 == 0:
                    act.activation(row, psum[:, bank:bank + 2, :], ACT.Gelu).then_inc(g_ready, 1)
                    return
                n = 2 * s + i // 2
                act.activation(row, psum[:, bank:bank + 2, :], ACT.Gelu, accum_out=g_sum[:, t:t + 1])\
                    .then_inc(g_ready, 1)
                act.wait_ge(g_ready, GROUP_TILES * s + i + 1)
                act.activation(g_minus_mean[:, t:t + 1], g_sum[:, t:t + 1], ACT.Copy, scale=-1.0 / HIDDEN)\
                    .then_inc(g_odd_mean, 1)
                act.wait_ge(g_odd_mean, n + 1)
                if n:
                    act.wait_ge(g_odd_square, n)
                act.activation(square_scratch[:, :], row, ACT.Square, bias=g_minus_mean[:, t:t + 1],
                               accum_out=g_square[:, t:t + 1]).then_inc(g_odd_square, 1)

            def g_hi(s, c):
                act.activation(gT_hi[:, c, :], full(("gT", c, order[s])), ACT.Copy, scale=ln_w[:, c:c + 1])\
                    .then_inc(gT_hi_ready, 1)

            act.preload_act_table(ACT.Sigmoid)
            for group in (1, 2):
                for k in range(DIM_CHUNKS):
                    xT_hi("xnT", xnT_hi, k, group)
            act.wait_ge(w_qkv_loaded, 16)
            w_hi(V)
            for t in range(IMAGE_TILES):
                bank = full(("embed", t))
                act.activation(h[:, t, :], bank[:, 0:DIM], ACT.Copy).then_inc(embed_ready, 1)
            w_hi(K)
            w_hi(Q)
            act.wait_ge(constants_loaded, 32)
            act.activation(row_weights_hi[:, :], columns[:, 12:28], ACT.Copy).then_inc(row_weight_hi_ready, 1)
            for k in range(DIM_CHUNKS):
                xT_hi("xnT", xnT_hi, k, 0)
            act.wait_ge(w_up_loaded, 16)
            act.activation(up_sign[:, :], w_up[:, :], ACT.Abs, accum_out=abs_sums[:, 0:1]).then_inc(abs_ready, 1)
            sigmoids(V, 0)
            sigmoids(V, 1)
            act.wait_ge(w_down_loaded, 16)
            act.activation(down_sign[:, :], w_down[:, :], ACT.Abs, accum_out=abs_sums[:, 1:2]).then_inc(abs_ready, 1)
            sigmoids(K, 0)
            act.wait_ge(w_proj_loaded, 16)
            act.activation(w_proj_hi[:, :, :], w_proj[:, :, :], ACT.Copy).then_inc(w_proj_hi_ready, 1)
            sigmoids(K, 1)
            for group in order:
                values(0, group)
            sigmoids(Q, 0)
            for group in order[:2]:
                values(1, group)
            sigmoids(Q, 1)
            act.preload_act_table(ACT.Gelu)
            values(1, order[2])
            for group in order:
                for c in range(DIM_CHUNKS):
                    att_hi(c, group)
            for k in range(DIM_CHUNKS):
                xT_hi("x2T", x2T_hi, k, order[0])
            for i in range(GROUP_TILES):
                gelu(0, i)
            for k in range(DIM_CHUNKS):
                xT_hi("x2T", x2T_hi, k, order[1])
            for s in range(1, GROUPS):
                for i in range(GROUP_TILES):
                    g_hi(s - 1, 2 * i)
                    g_hi(s - 1, 2 * i + 1)
                    if i:
                        gelu(s, i - 1)
                gelu(s, GROUP_TILES - 1)
                if s + 1 < GROUPS:
                    for k in range(DIM_CHUNKS):
                        xT_hi("x2T", x2T_hi, k, order[s + 1])
            for c in range(HIDDEN_CHUNKS):
                g_hi(GROUPS - 1, c)

        @blk.gpsimd
        def _(pool):
            pool.memset(minus_half[:, :], -0.5).then_inc(pool_constants, 1)
            pool.memset(ones[:, :], 1.0).then_inc(pool_constants, 1)
            pool.wait_ge(pool_constants, 2)

            def norm_rsqrt(layer, n, group):
                pool.wait_ge(norm_var_ready, n)
                ts = slice(GROUP_TILES * group, GROUP_TILES * (group + 1))
                pool.tensor_tensor(norm_rstd[:, layer, ts], norm_var[:, layer, ts], minus_half[:, :], ALU.pow)\
                    .then_inc(norm_rstd_ready, 1)

            def bn_rsqrt(j):
                pool.wait_ge(bn_var_ready, j + 1)
                pool.tensor_tensor(bn_rstd[:, j:j + 1], bn_var[:, j:j + 1], minus_half[:, 0:1], ALU.pow)\
                    .then_inc(bn_rstd_ready, 1)

            def add_bias(n, group):
                pool.wait_ge(xn_ready, GROUP_TILES * (n + 1))
                for t in tiles_of(group):
                    pool.tensor_tensor(h[:, t, :], h[:, t, :], proj_bias[:, :], ALU.add).then_inc(biased, 1)

            def g_rsqrt(s):
                ts = slice(GROUP_TILES * order[s], GROUP_TILES * (order[s] + 1))
                pool.wait_ge(g_var_ready, 2 * (s + 1))
                pool.tensor_tensor(g_rstd[:, ts], g_var[:, ts], minus_half[:, :], ALU.pow).then_inc(g_rstd_ready, 1)

            def shift_h2(s):
                pool.wait_ge(xn_ready, TILES + GROUP_TILES * (s + 1))
                pool.wait_ge(rows_ready, 1)
                for t in tiles_of(order[s]):
                    pool.tensor_tensor(h[:, t, :], h[:, t, :], rows[:, 1, :], ALU.add).then_inc(h2_shifted, 1)

            def subtract_mean(s):
                g_rsqrt(s)
                ts = slice(GROUP_TILES * order[s], GROUP_TILES * (order[s] + 1))
                pool.wait_ge(g_rstd_ready, s + 1)
                pool.wait_ge(g_mean_ready, s + 1)
                pool.tensor_tensor(g_mean_slope[:, ts], g_minus_mean[:, ts], g_rstd[:, ts], ALU.mult)\
                    .then_inc(g_mean_slope_ready, 1)
                pool.wait_ge(g_mean_slope_ready, s + 1)
                pool.wait_ge(h2_shifted, GROUP_TILES * (s + 1))
                for i, t in enumerate(tiles_of(order[s])):
                    n = GROUP_TILES * s + i
                    if n:
                        pool.wait_ge(h2_complete, n)
                    pool.tensor_scalar(row_term[:, :], rows[:, 0, :], g_mean_slope[:, t:t + 1], None, ALU.mult)\
                        .then_inc(row_term_ready, 1)
                    pool.wait_ge(row_term_ready, n + 1)
                    pool.tensor_tensor(h[:, t, :], h[:, t, :], row_term[:, :], ALU.add).then_inc(h2_complete, 1)

            def ternary_down(i):
                part = slice(512 * i, 512 * (i + 1))
                if i:
                    pool.wait_ge(down_ready, i)
                pool.tensor_scalar(positive[:, :], w_down[:, part], thresholds[:, 0, 1:2], None, ALU.is_gt)\
                    .then_inc(down_part, 1)
                pool.tensor_scalar(negative[:, :], w_down[:, part], thresholds[:, 1, 1:2], None, ALU.is_lt)\
                    .then_inc(down_part, 1)
                pool.wait_ge(down_part, 2 * i + 2)
                pool.tensor_tensor(down_sign[:, part], positive[:, :], negative[:, :], ALU.subtract)\
                    .then_inc(down_ready, 1)

            norm_rsqrt(0, 1, 1)
            norm_rsqrt(0, 2, 2)
            norm_rsqrt(0, 3, 0)
            pool.wait_ge(constants_loaded, 32)
            add_bias(0, 1)
            add_bias(1, 2)
            bn_rsqrt(0)
            bn_rsqrt(1)
            add_bias(2, 0)
            bn_rsqrt(2)
            bn_rsqrt(3)
            pool.wait_ge(threshold_ready, 2)
            ternary_down(0)
            bn_rsqrt(4)
            bn_rsqrt(5)
            for n, group in enumerate(order):
                pool.wait_ge(sigmoid_ready, GROUPS * qkv_index(Q, 0) + n + 1)
                q = act_qkv[:, qkv_index(Q, 0), cols(group)]
                pool.tensor_tensor(q, q, act_qkv[:, qkv_index(K, 0), cols(group)], ALU.mult).then_inc(qk0_ready, 1)
            for i in range(1, 4):
                ternary_down(i)
            for s in range(GROUPS):
                norm_rsqrt(1, GROUPS + s + 1, order[s])
            shift_h2(0)
            subtract_mean(0)
            shift_h2(1)
            shift_h2(2)
            subtract_mean(1)
            subtract_mean(2)

        @blk.vector
        def _(dve):
            def full(what):
                dve.wait_ge(bank_full[BANK[what]], nth[what])
                return psum[:, BANK[what], :]

            def norm_statistics(layer, n, group):
                for i, t in enumerate(tiles_of(group)):
                    dve.bn_stats(norm_stats[:, layer, t, :], h[:, t, :]).then_inc(norm_stat, 1)
                for i, t in enumerate(tiles_of(group)):
                    dve.wait_ge(norm_stat, GROUP_TILES * n + i + 1)
                    dve.bn_aggr(norm_moments[:, layer, t, :], norm_stats[:, layer, t, :]).then_inc(norm_moment, 1)
                dve.wait_ge(norm_moment, GROUP_TILES * (n + 1))
                ts = slice(GROUP_TILES * group, GROUP_TILES * (group + 1))
                dve.tensor_scalar(norm_var[:, layer, ts], norm_moments[:, layer, ts, 1], NORM_EPS, None, ALU.add)\
                    .then_inc(norm_var_ready, 1)

            def normalise(layer, n, group):
                dve.wait_ge(norm_rstd_ready, n + 1)
                for t in tiles_of(group):
                    dve.tensor_scalar(xn[:, t, :], h[:, t, :], norm_moments[:, layer, t, 0:1],
                                      norm_rstd[:, layer, t:t + 1], ALU.subtract, ALU.mult).then_inc(xn_ready, 1)

            def w_lo(m):
                e = slice(DIM * m, DIM * (m + 1))
                dve.wait_ge(w_qkv_hi_ready, m + 1)
                dve.tensor_tensor(w_qkv_lo[:, :, e], w_qkv[:, :, e], w_qkv_hi[:, :, e].bitcast(fp32), ALU.subtract)\
                    .then_inc(w_qkv_lo_ready, 1)

            def xT_lo(kind, hi, lo, n, k, group):
                dve.wait_ge(xT_hi_ready, n + 1)
                dve.tensor_tensor(lo[:, k, cols(group)], psum[:, BANK[(kind, k, group)], :],
                                  hi[:, k, cols(group)].bitcast(fp32), ALU.subtract)\
                    .then_inc(xT_lo_ready, 1)

            qkv_stats = []

            def qkv_statistics(m, c, group):
                j = qkv_index(m, c)
                dve.bn_stats(bn_stats[:, j, 6 * group:6 * (group + 1)], full(("qkv", m, c, group)))\
                    .then_inc(bn_stat, 1)
                qkv_stats.append((m, c, group))

            def qkv_affine(m, c):
                j = qkv_index(m, c)
                dve.wait_ge(bn_stat, len(qkv_stats))
                dve.bn_aggr(bn_moments[:, j, :], bn_stats[:, j, :]).then_inc(bn_moment, 1)
                dve.wait_ge(bn_moment, j + 1)
                dve.tensor_scalar(bn_var[:, j:j + 1], bn_moments[:, j, 1:2], NORM_EPS, None, ALU.add)\
                    .then_inc(bn_var_ready, 1)

            def qkv_affine_end(m, c):
                j = qkv_index(m, c)
                dve.wait_ge(bn_rstd_ready, j + 1)
                dve.tensor_tensor(bn_slope[:, j:j + 1], bn_rstd[:, j:j + 1], bn_gain[:, j:j + 1], ALU.mult)\
                    .then_inc(bn_slopes, 1)
                dve.tensor_tensor(bn_minus_slope[:, j:j + 1], bn_rstd[:, j:j + 1], bn_minus_gain[:, j:j + 1], ALU.mult)\
                    .then_inc(bn_slopes, 1)
                dve.wait_ge(bn_slopes, 2 * (j + 1))
                dve.scalar_tensor_tensor(bn_shift[:, j:j + 1], bn_moments[:, j, 0:1], bn_minus_slope[:, j:j + 1],
                                         bn_offset[:, j:j + 1], ALU.mult, ALU.add).then_inc(bn_ready, 1)

            def gram_scaled(c, half):
                what = ("gram", c, half)
                bank = full(what).rearrange("p (b e) -> p b e", b=4)
                mask = head_mask.rearrange("p (a e) -> p a e", a=1).broadcast_to([P, 4, P])
                dve.tensor_tensor(gram[:, c, 4 * half:4 * (half + 1), :], bank, mask, ALU.mult)\
                    .then_inc(gram_ready, 1)

            def att_lo(n, c, group):
                dve.wait_ge(att_hi_ready, n + 1)
                dve.tensor_tensor(attT_lo[:, c, cols(group)], psum[:, BANK[("mix", c, group)], :],
                                  attT_hi[:, c, cols(group)].bitcast(fp32), ALU.subtract)\
                    .then_inc(att_lo_ready, 1)

            def residual(s):
                for pair in range(2):
                    t0 = GROUP_TILES * order[s] + 2 * pair
                    what = ("proj", t0)
                    bank = full(what).rearrange("p (t d) -> p t d", t=2)
                    dve.tensor_tensor(h[:, t0:t0 + 2, :], bank, h[:, t0:t0 + 2, :], ALU.add)\
                        .then_inc(h2_ready, 1)
                dve.wait_ge(h2_ready, 2 * (s + 1))

            def second_norm(s):
                residual(s)
                norm_statistics(1, GROUPS + s, order[s])

            def x2T_lo(s):
                for k in range(DIM_CHUNKS):
                    xT_lo("x2T", x2T_hi, x2T_low, DIM_CHUNKS * (GROUPS + s) + k, k, order[s])

            def g_statistics(s, i):
                t = GROUP_TILES * order[s] + i
                n = 2 * s + i // 2
                dve.wait_ge(g_ready, GROUP_TILES * s + i + 1)
                for half in range(2):
                    dve.bn_stats(g_stats[:, t, half, :], g[:, GROUP_TILES * (s % 2) + i, 512 * half:512 * (half + 1)])\
                        .then_inc(g_stat, 1)
                dve.wait_ge(g_stat, 2 * (n + 1))
                dve.bn_aggr(g_moments[:, t, :], g_stats[:, t, :, :].rearrange("p a b -> p (a b)")).then_inc(g_moment, 1)

            def g_moments_done(s):
                first = GROUP_TILES * order[s]
                even, odd = slice(first, first + GROUP_TILES, 2), slice(first + 1, first + GROUP_TILES, 2)
                dve.wait_ge(g_odd_square, 2 * (s + 1))
                dve.tensor_scalar(g_var[:, odd], g_square[:, odd], 1.0 / HIDDEN, NORM_EPS, ALU.mult, ALU.add)\
                    .then_inc(g_var_ready, 1)
                dve.wait_ge(g_moment, 2 * (s + 1))
                dve.tensor_scalar(g_var[:, even], g_moments[:, even, 1], NORM_EPS, None, ALU.add).then_inc(g_var_ready, 1)
                dve.tensor_scalar(g_minus_mean[:, even], g_moments[:, even, 0], -1.0, None, ALU.mult)\
                    .then_inc(g_mean_ready, 1)

            def g_lo(s, c):
                dve.wait_ge(gT_hi_ready, HIDDEN_CHUNKS * s + c + 1)
                what = ("gT", c, order[s])
                dve.scalar_tensor_tensor(gT_lo[:, c, :], psum[:, BANK[what], :], ln_w[:, c:c + 1],
                                         gT_hi[:, c, :].bitcast(fp32), ALU.mult, ALU.subtract)\
                    .then_inc(gT_lo_ready, 1)

            def finish(s, i):
                t = GROUP_TILES * order[s] + i
                n = GROUP_TILES * s + i
                bank = full(("down", t))
                dve.wait_ge(h2_complete, n + 1)
                dve.scalar_tensor_tensor(h[:, t, :], bank[:, 0:DIM], g_rstd[:, t:t + 1], h[:, t, :],
                                         ALU.mult, ALU.add).then_inc(final_ready, 1)

            dve.wait_ge(text_loaded[0], 16)
            norm_statistics(0, 0, 1)
            dve.wait_ge(text_loaded[1], 16)
            norm_statistics(0, 1, 2)
            normalise(0, 0, 1)
            normalise(0, 1, 2)
            for n, (group, k) in enumerate([(1, 0), (1, 1), (2, 0), (2, 1)]):
                xT_lo("xnT", xnT_hi, xnT_lo, n, k, group)
            w_lo(V)
            dve.wait_ge(embed_ready, IMAGE_TILES)
            norm_statistics(0, 2, 0)
            w_lo(K)
            normalise(0, 2, 0)
            qkv_statistics(V, 0, 1)
            qkv_statistics(V, 0, 2)
            for k in range(DIM_CHUNKS):
                xT_lo("xnT", xnT_hi, xnT_lo, 4 + k, k, 0)
            qkv_statistics(V, 1, 1)
            qkv_statistics(V, 1, 2)
            dve.wait_ge(constants_loaded, 32)
            dve.tensor_scalar(bn_gain[:, :], gain4, SIGMOID_SLOPE, None, ALU.mult).then_inc(bn_constants, 1)
            dve.tensor_scalar(bn_minus_gain[:, :], gain4, -SIGMOID_SLOPE, None, ALU.mult).then_inc(bn_constants, 1)
            dve.tensor_scalar(bn_offset[:, :], shift, V_THRESHOLD, SIGMOID_SLOPE, ALU.subtract, ALU.mult)\
                .then_inc(bn_constants, 1)
            w_lo(Q)
            dve.wait_ge(bn_constants, 3)
            qkv_statistics(V, 0, 0)
            qkv_affine(V, 0)
            dve.wait_ge(row_weight_hi_ready, 1)
            dve.tensor_tensor(row_weights_lo[:, :], columns[:, 12:28], row_weights_hi[:, :].bitcast(fp32),
                              ALU.subtract).then_inc(row_weight_ready, 1)
            qkv_affine_end(V, 0)
            qkv_statistics(V, 1, 0)
            qkv_affine(V, 1)
            qkv_affine_end(V, 1)
            for group in order:
                qkv_statistics(K, 0, group)
            qkv_affine(K, 0)
            qkv_affine_end(K, 0)
            for group in order:
                qkv_statistics(K, 1, group)
            qkv_affine(K, 1)
            dve.wait_ge(w_proj_hi_ready, 1)
            dve.tensor_tensor(w_proj_lo[:, :, :], w_proj[:, :, :], w_proj_hi[:, :, :].bitcast(fp32), ALU.subtract)\
                .then_inc(w_proj_lo_ready, 1)
            qkv_affine_end(K, 1)
            bank = full(("absmean",))
            dve.tensor_scalar(absmeans[:, :], bank[:, 0:2], 1.0 / (DIM * HIDDEN), ABSMEAN_EPS, ALU.mult, ALU.add)\
                .then_inc(absmean_ready, 1)
            dve.wait_ge(absmean_ready, 1)
            dve.tensor_scalar(thresholds[:, 0, :], absmeans[:, :], 0.5, None, ALU.mult).then_inc(threshold_ready, 1)
            dve.tensor_scalar(thresholds[:, 1, :], absmeans[:, :], -0.5, None, ALU.mult).then_inc(threshold_ready, 1)
            dve.wait_ge(threshold_ready, 2)
            dve.tensor_scalar(up_negative[:, :], w_up[:, :], thresholds[:, 1, 0:1], None, ALU.is_lt)\
                .then_inc(up_part, 1)
            for group in order:
                qkv_statistics(Q, 0, group)
            qkv_affine(Q, 0)
            qkv_affine_end(Q, 0)
            for n, group in enumerate(order):
                qkv_statistics(Q, 1, group)
            qkv_affine(Q, 1)
            qkv_affine_end(Q, 1)
            dve.wait_ge(up_part, 1)
            dve.scalar_tensor_tensor(up_sign[:, :], w_up[:, :], thresholds[:, 0, 0:1], up_negative[:, :],
                                     ALU.is_gt, ALU.subtract).then_inc(up_ready, 1)
            for n, group in enumerate(order):
                dve.wait_ge(sigmoid_ready, GROUPS * qkv_index(Q, 1) + n + 1)
                q = act_qkv[:, qkv_index(Q, 1), cols(group)]
                dve.tensor_tensor(q, q, act_qkv[:, qkv_index(K, 1), cols(group)], ALU.mult).then_inc(qk1_ready, 1)
            for c in range(DIM_CHUNKS):
                for half in range(2):
                    gram_scaled(c, half)
            for n in range(2 * DIM_CHUNKS):
                att_lo(n, n % DIM_CHUNKS, order[n // DIM_CHUNKS])
            dve.wait_ge(biased, TILES)
            second_norm(0)
            for n in range(2 * DIM_CHUNKS, 3 * DIM_CHUNKS):
                att_lo(n, n % DIM_CHUNKS, order[n // DIM_CHUNKS])
            normalise(1, GROUPS, order[0])
            second_norm(1)
            bank = full(("ffn_rows",))
            dve.tensor_copy(rows[:, :, :], bank.rearrange("p (r d) -> p r d", r=2)).then_inc(rows_ready, 1)
            x2T_lo(0)
            normalise(1, GROUPS + 1, order[1])
            second_norm(2)
            x2T_lo(1)
            normalise(1, GROUPS + 2, order[2])
            for s in range(1, GROUPS):
                for c in range(HIDDEN_CHUNKS):
                    g_lo(s - 1, c)
                    if c % 4 == 1:
                        g_statistics(s - 1, c // 2)
                g_moments_done(s - 1)
                if s + 1 < GROUPS:
                    x2T_lo(s + 1)
                for i in range(GROUP_TILES):
                    finish(s - 1, i)
            for i in (0, 2):
                g_statistics(GROUPS - 1, i)
            g_moments_done(GROUPS - 1)
            for c in range(HIDDEN_CHUNKS):
                g_lo(GROUPS - 1, c)
            for i in range(GROUP_TILES):
                finish(GROUPS - 1, i)


_SHAPE = (TILES, P, DIM)


def kernel(**inputs):
    import concourse.bacc as _bacc
    from concourse.bass_utils import run_bass_kernel_spmd as _run

    a = {k: np.asarray(v) for k, v in inputs.items()}

    def feature_major(m, chunks):
        return np.ascontiguousarray(m.reshape(chunks, P, -1).transpose(1, 0, 2))

    side = a["x"].shape[1] // PATCH
    image = a["x"].reshape(BATCHES, side, PATCH, side, PATCH, 3).transpose(2, 4, 5, 0, 1, 3)
    image = image.reshape(PATCH_FEATURES, BATCHES * IMAGE_TOKENS)
    w_qkv = np.concatenate([a["L0_attn_Wv"].T, a["L0_attn_Wk"].T, a["L0_attn_Wq"].T], axis=1)
    halves = np.zeros((P, 2), np.float32)
    halves[:64, 0] = 1.0
    halves[64:, 1] = 1.0
    columns = np.concatenate(
        [a[f"L0_attn_{n}{m}"].reshape(2, P).T for n in "gb" for m in "vkq"]
        + [a["L0_ffn_ln_w"].reshape(8, P).T, a["L0_ffn_ln_b"].reshape(8, P).T, halves], axis=1)
    head = np.arange(P) // HEAD_DIM
    squares = np.concatenate(
        [np.eye(P, dtype=np.float32),
         np.where(head[:, None] == head[None, :], np.float32(HEAD_DIM ** -0.5), np.float32(0))], axis=1)
    arrays = {
        "embed_in": np.concatenate([feature_major(image, PATCH_CHUNKS), feature_major(a["L0_tok_W"], PATCH_CHUNKS)],
                                   axis=2),
        "text_in": np.ascontiguousarray(a["txt"].transpose(1, 0, 2)),
        "w_qkv_in": feature_major(w_qkv, DIM_CHUNKS),
        "w_proj_in": feature_major(a["L0_attn_Wp"].T, DIM_CHUNKS),
        "w_up_in": feature_major(a["L0_ffn_W_fc"].T, DIM_CHUNKS).reshape(P, -1),
        "w_down_in": feature_major(a["L0_ffn_W_proj"].T, HIDDEN_CHUNKS).reshape(P, -1),
        "columns_in": np.ascontiguousarray(columns),
        "proj_bias_in": a["L0_attn_bp"],
        "squares_in": np.ascontiguousarray(squares),
    }
    nc = _bacc.Bacc("TRN2", target_bir_lowering=False, num_devices=1)
    args = {n: nc.dram_tensor(n, v.shape, mybir.dt.from_np(v.dtype), kind="ExternalInput").ap()
            for n, v in arrays.items()}
    out = nc.dram_tensor("out", _SHAPE, mybir.dt.float32, kind="ExternalOutput").ap()
    block(nc, *args.values(), out)
    r = _run(nc, [arrays], core_ids=[0]).results[0]["out"]
    result = np.empty((BATCHES, IMAGE_TOKENS + TEXT_TOKENS, DIM), r.dtype)
    result[:, :IMAGE_TOKENS] = r[:IMAGE_TILES].reshape(BATCHES, IMAGE_TOKENS, DIM)
    result[:, IMAGE_TOKENS:] = r[IMAGE_TILES:]
    return result
```

```python
import numpy as np
import concourse.bass as bass
from concourse import mybir
from contextlib import ExitStack

P = 128
BATCHES, IMAGE_TOKENS, TEXT_TOKENS = 8, 64, 128
DIM, HEADS, HIDDEN = 256, 16, 1024
HEAD_DIM = DIM // HEADS
PATCH = 16
PATCH_FEATURES = 3 * PATCH * PATCH
TOKENS = BATCHES * (IMAGE_TOKENS + TEXT_TOKENS)
TILES = TOKENS // P
IMAGE_TILES = BATCHES * IMAGE_TOKENS // P
GROUP_TILES = 4
GROUP = GROUP_TILES * P
GROUPS = TILES // GROUP_TILES
DIM_CHUNKS = DIM // P
HIDDEN_CHUNKS = HIDDEN // P
PATCH_CHUNKS = PATCH_FEATURES // P
NORM_EPS = 1e-5
ABSMEAN_EPS = 1e-6
V_THRESHOLD, SIGMOID_SLOPE = 1.0, 4.0
V, K, Q = 0, 1, 2

GROUP_ORDER = (1, 2, 0)
WARM_UP_PRODUCTS = 6
EMBED_SPLIT = (4, 5)
STATISTICS_AFTER = (((3,), (4,), (), (5,)), ((6, 7), (8,), (9,), (10,)), ((11,), (), (), ()))


def bank_uses():
    uses = []
    first, second, image = GROUP_ORDER

    def use(what, bank):
        uses.append((what, bank))

    def use_groups(kind, index, banks):
        for group, bank in zip(GROUP_ORDER, banks):
            use((kind, *index, group), bank)

    for t in range(IMAGE_TILES):
        use(("embed", t), t)
    for n, group in enumerate((first, second)):
        for k in range(DIM_CHUNKS):
            use(("xnT", k, group), 4 + 2 * n + k)
    use(("qkv", V, 0, first), 4)
    use(("qkv", V, 0, second), 5)
    use(("qkv", V, 1, first), 6)
    for k in range(DIM_CHUNKS):
        use(("xnT", k, image), k)
    use(("qkv", V, 1, second), 7)
    for c in range(DIM_CHUNKS):
        use(("qkv", V, c, image), c)
    use(("qkv", K, 0, first), 2)
    use(("qkv", K, 0, second), 3)
    use(("qkv", K, 0, image), 4)
    use(("absmean",), 5)
    use_groups("qkv", (K, 1), (0, 6, 7))
    use(("valueT", 0, first), 1)
    use(("valueT", 0, second), 5)
    use(("qkv", Q, 0, first), 2)
    use(("qkv", Q, 0, second), 3)
    use(("valueT", 0, image), 1)
    use(("valueT", 1, first), 5)
    use(("qkv", Q, 0, image), 4)
    use(("qkv", Q, 1, first), 0)
    use(("valueT", 1, second), 1)
    use(("qkv", Q, 1, second), 6)
    use(("valueT", 1, image), 5)
    use(("qkv", Q, 1, image), 7)
    for c in range(DIM_CHUNKS):
        for half in range(2):
            use(("gram", c, half), ((1, 5), (2, 3))[c][half])
    use(("mix", 0, first), 4)
    use(("mix", 1, first), 6)
    use(("mix", 0, second), 0)
    use(("mix", 1, second), 7)

    def proj(group, pair, bank):
        use(("proj", GROUP_TILES * group + 2 * pair), bank)

    def x2T(group, banks):
        for k, bank in enumerate(banks):
            use(("x2T", k, group), bank)

    def up(group, i):
        use(("up", GROUP_TILES * group + i), 2 * (i % 2))

    def gT(group, i, bank=4):
        for c in (2 * i, 2 * i + 1):
            use(("gT", c, group), bank + c % 2)

    proj(first, 0, 1)
    proj(first, 1, 5)
    use(("mix", 0, image), 2)
    use(("mix", 1, image), 3)
    proj(second, 0, 4)
    proj(second, 1, 0)
    proj(image, 0, 6)
    x2T(first, (4, 5))
    proj(image, 1, 7)
    use(("ffn_rows",), 3)
    up(first, 0)
    up(first, 1)
    x2T(second, (6, 7))
    up(first, 2)
    up(first, 3)
    up(second, 0)
    for i in range(GROUP_TILES):
        gT(first, i, (4, 6, 6, 4)[i])
        if i + 1 < GROUP_TILES:
            up(second, i + 1)
        if i == 1:
            x2T(image, (4, 5))
    up(image, 0)
    for i in range(GROUP_TILES):
        gT(second, i)
        if i + 1 < GROUP_TILES:
            up(image, i + 1)
        use(("down", GROUP_TILES * first + i), 6 + i % 2)
    gT(image, 0)
    for i in range(GROUP_TILES):
        if i + 1 < GROUP_TILES:
            gT(image, i + 1, (0, 4, 0)[i])
        use(("down", GROUP_TILES * second + i), (6, 7, 2, 3)[i])
    for i in range(GROUP_TILES):
        use(("down", GROUP_TILES * image + i), (6, 7, 4, 5)[i])
    return uses


def block(
    nc, embed_in, text_in, w_qkv_in, w_proj_in, w_up_in, w_down_in,
    columns_in, proj_bias_in, squares_in, out,
):
    fp32, fp32r = mybir.dt.float32, mybir.dt.float32r
    ALU, ACT = mybir.AluOpType, mybir.ActivationFunctionType

    with ExitStack() as ctx:
        def sem(name):
            return ctx.enter_context(nc.semaphore(name))

        offset = [nc.sbuf_base]
        floats = 4

        def place(name, shape, dt=fp32, at=None):
            size = int(np.prod(shape[1:])) * floats
            if at is None:
                at = -(-offset[0] // 32) * 32
                offset[0] = at + size
            return nc.alloc_sbuf_tensor_at(name, shape, dt, offset=at), at, at + size

        h, _, _ = place("h", [P, TILES, DIM])
        xn, at_xn, _ = place("xn", [P, TILES, DIM])
        xnT_hi, at_xnT, _ = place("xnT_hi", [P, DIM_CHUNKS, TOKENS], fp32r)
        xnT_lo, at_xnT_lo, _ = place("xnT_lo", [P, DIM_CHUNKS, TOKENS], fp32r)
        attT_hi, _, _ = place("attT_hi", [P, DIM_CHUNKS, TOKENS], fp32r, at_xnT)
        attT_lo, _, _ = place("attT_lo", [P, DIM_CHUNKS, TOKENS], fp32r, at_xnT_lo)
        x2T_hi, at_x2T, _ = place("x2T_hi", [P, DIM_CHUNKS, TOKENS], fp32r)
        x2T_low, _, _ = place("x2T_low", [P, DIM_CHUNKS, TOKENS], fp32r)
        embed, _, _ = place("embed", [P, PATCH_CHUNKS, GROUP + DIM], fp32, at_x2T)
        act_qkv, at_qkv, _ = place("act_qkv", [P, 3 * DIM_CHUNKS, TOKENS])
        embed_hi, _, after = place("embed_hi", [P, len(EMBED_SPLIT), GROUP + DIM], fp32r, at_qkv)
        embed_lo, _, _ = place("embed_lo", [P, len(EMBED_SPLIT), GROUP + DIM], fp32r, after)
        gT_hi, gT_lo = [], []
        for n, at in enumerate((at_qkv, at_xn)):
            part, _, after = place(f"gT_hi{n}", [P, HIDDEN_CHUNKS, GROUP], fp32r, at)
            gT_hi.append(part)
            part, _, _ = place(f"gT_lo{n}", [P, HIDDEN_CHUNKS, GROUP], fp32r, after)
            gT_lo.append(part)
        g, at_g, _ = place("g", [P, 2 * GROUP_TILES, HIDDEN])
        v_text, _, after = place("v_text", [P, DIM_CHUNKS, BATCHES, P], fp32, at_g)
        v_image, _, after = place("v_image", [P, DIM_CHUNKS, 2, IMAGE_TILES, P], fp32, after)
        gram, _, after = place("gram", [P, DIM_CHUNKS, BATCHES, P], fp32, after)
        w_qkv, _, after = place("w_qkv", [P, DIM_CHUNKS, 3 * DIM], fp32, after)
        w_proj, _, _ = place("w_proj", [P, DIM_CHUNKS, DIM], fp32, after)
        w_qkv_hi, _, _ = place("w_qkv_hi", [P, DIM_CHUNKS, 3 * DIM], fp32r)
        w_qkv_lo, _, _ = place("w_qkv_lo", [P, DIM_CHUNKS, 3 * DIM], fp32r)
        w_proj_hi, _, _ = place("w_proj_hi", [P, DIM_CHUNKS, DIM], fp32r)
        w_proj_lo, _, _ = place("w_proj_lo", [P, DIM_CHUNKS, DIM], fp32r)
        w_up, _, _ = place("w_up", [P, DIM_CHUNKS * HIDDEN])
        w_down, _, _ = place("w_down", [P, HIDDEN_CHUNKS * DIM])
        up_sign, _, _ = place("up_sign", [P, DIM_CHUNKS * HIDDEN], fp32r)
        down_sign, _, _ = place("down_sign", [P, HIDDEN_CHUNKS * DIM], fp32r)
        up_negative, _, after = place("up_negative", [P, DIM_CHUNKS * HIDDEN], fp32, at_x2T)
        negative, _, after = place("negative", [P, 512], fp32, after)
        positive, _, _ = place("positive", [P, 512], fp32, after)
        squares, _, _ = place("squares", [P, 2 * P])
        columns, _, _ = place("columns", [P, 31])
        proj_bias, _, _ = place("proj_bias", [P, DIM])
        ones, _, _ = place("ones", [P, P])
        minus_half, _, _ = place("minus_half", [P, GROUP_TILES])
        row_parts, _, _ = place("row_parts", [4, DIM])
        spread_parts, _, _ = place("spread_parts", [P, 4, DIM])
        rows, _, _ = place("rows", [P, 2, DIM])
        row_weights, _, _ = place("row_weights", [P, HIDDEN_CHUNKS, 4], fp32r)
        norm_stats, _, _ = place("norm_stats", [P, 2, TILES, 6])
        norm_moments, _, _ = place("norm_moments", [P, 2, TILES, 2])
        norm_var, _, _ = place("norm_var", [P, 2, TILES])
        norm_rstd, _, _ = place("norm_rstd", [P, 2, TILES])
        bn_stats, _, _ = place("bn_stats", [P, 3 * DIM_CHUNKS, GROUPS * 6])
        bn_moments, _, _ = place("bn_moments", [P, 3 * DIM_CHUNKS, 2])
        bn_var, _, _ = place("bn_var", [P, 3 * DIM_CHUNKS])
        bn_rstd, _, _ = place("bn_rstd", [P, 3 * DIM_CHUNKS])
        bn_slope, _, _ = place("bn_slope", [P, 3 * DIM_CHUNKS])
        bn_minus_slope, _, _ = place("bn_minus_slope", [P, 3 * DIM_CHUNKS])
        bn_shift, _, _ = place("bn_shift", [P, 3 * DIM_CHUNKS])
        g_stats, _, _ = place("g_stats", [P, TILES, 2, 6])
        g_moments, _, _ = place("g_moments", [P, TILES, 2])
        g_var, _, _ = place("g_var", [P, TILES])
        g_rstd, _, _ = place("g_rstd", [P, TILES])
        abs_sums, _, _ = place("abs_sums", [P, 2])
        absmeans, _, _ = place("absmeans", [P, 2])
        thresholds, _, _ = place("thresholds", [P, 2, 2])
        g_mean_slope, _, _ = place("g_mean_slope", [P, TILES])
        row_term, _, _ = place("row_term", [P, DIM])

        identity, head_mask = squares[:, 0:P], squares[:, P:2 * P]
        gain4 = columns[:, 0:6]
        shift = columns[:, 6:12]
        hidden_affine = columns[:, 12:28].rearrange("p (c r) -> p c r", r=2)
        ln_w = columns[:, 12:28:2]
        row_sign = columns[0:4, 30:31]
        half_mask = (columns[:, 28:29], columns[:, 29:30])
        bn_gain, _, _ = place("bn_gain", [P, 6])
        bn_minus_gain, _, _ = place("bn_minus_gain", [P, 6])
        bn_offset, _, _ = place("bn_offset", [P, 6])
        assert offset[0] <= nc.sbuf_usable_end, offset[0]

        psum = ctx.enter_context(nc.psum_tensor("psum", [P, 8, 512], fp32))

        order = GROUP_ORDER

        def tiles_of(group):
            return range(GROUP_TILES * group, GROUP_TILES * (group + 1))

        nth, BANK, BEFORE = {}, {}, {}
        held = [[] for _ in range(8)]

        def hold(what, bank):
            BEFORE[what] = held[bank][-1] if held[bank] else None
            held[bank].append(what)
            nth[what], BANK[what] = len(held[bank]), bank

        for what, bank in bank_uses():
            hold(what, bank)
            if what[0] == "up":
                hold(("up2", what[1]), bank + 1)

        bank_full = [sem(f"bank_full{b}") for b in range(8)]

        text_loaded = [sem("text_loaded_g1"), sem("text_loaded_g2")]
        w_v_loaded, w_kq_loaded = sem("w_v_loaded"), sem("w_kq_loaded")
        constants_loaded = sem("constants_loaded")
        embed_loaded = [sem(f"embed_loaded{f}") for f in range(PATCH_CHUNKS)]
        embed_hi_ready, embed_lo_ready = sem("embed_hi_ready"), sem("embed_lo_ready")
        identity_loaded = sem("identity_loaded")
        w_proj_loaded = sem("w_proj_loaded")
        w_up_loaded = sem("w_up_loaded")
        w_down_loaded = sem("w_down_loaded")
        out_stored = sem("out_stored")
        w_qkv_hi_ready, w_qkv_lo_ready = sem("w_qkv_hi_ready"), sem("w_qkv_lo_ready")
        w_proj_hi_ready, w_proj_lo_ready = sem("w_proj_hi_ready"), sem("w_proj_lo_ready")
        pool_constants = sem("pool_constants")
        norm_stat, norm_moment = sem("norm_stat"), sem("norm_moment")
        norm_var_ready, norm_rstd_ready = sem("norm_var_ready"), sem("norm_rstd_ready")
        xn_ready = sem("xn_ready")
        xT_hi_ready, xT_lo_ready = sem("xT_hi_ready"), sem("xT_lo_ready")
        bn_constants = sem("bn_constants")
        bn_stat, bn_moment = sem("bn_stat"), sem("bn_moment")
        bn_var_ready, bn_rstd_ready = sem("bn_var_ready"), sem("bn_rstd_ready")
        bn_slopes, bn_ready = sem("bn_slopes"), sem("bn_ready")
        sigmoid_ready = sem("sigmoid_ready")
        abs_ready, absmean_ready, threshold_ready = sem("abs_ready"), sem("absmean_ready"), sem("threshold_ready")
        up_part, down_part = sem("up_part"), sem("down_part")
        up_ready, down_ready = sem("up_ready"), sem("down_ready")
        value_ready, gram_ready = sem("value_ready"), sem("gram_ready")
        qk_text_ready, qk_image_ready = sem("qk_text_ready"), sem("qk_image_ready")
        att_hi_ready, att_lo_ready = sem("att_hi_ready"), sem("att_lo_ready")
        embed_ready, biased = sem("embed_ready"), sem("biased")
        h2_ready, h2_shifted = sem("h2_ready"), sem("h2_shifted")
        row_weight_hi_ready, row_weight_ready = sem("row_weight_hi_ready"), sem("row_weight_ready")
        row_parts_ready, rows_spread, rows_ready = sem("row_parts_ready"), sem("rows_spread"), sem("rows_ready")
        g_ready = sem("g_ready")
        g_stat, g_moment = sem("g_stat"), sem("g_moment")
        g_var_ready, g_rstd_ready = sem("g_var_ready"), sem("g_rstd_ready")
        gT_hi_ready, gT_lo_ready = sem("gT_hi_ready"), sem("gT_lo_ready")
        final_ready = sem("final_ready")
        g_mean_slope_ready, row_term_ready = sem("g_mean_slope_ready"), sem("row_term_ready")
        h2_complete = sem("h2_complete")
        final_order = [GROUP_TILES * gr + i for gr in order for i in range(GROUP_TILES)]


        def place_of(t):
            return GROUP_TILES * order.index(t // GROUP_TILES) + t % GROUP_TILES

        def was_read(what):
            kind, *at = what
            if kind == "xnT":
                k, group = at
                return xT_lo_ready, DIM_CHUNKS * order.index(group) + k + 1
            if kind == "x2T":
                k, group = at
                return xT_lo_ready, DIM_CHUNKS * (GROUPS + order.index(group)) + k + 1
            if kind == "embed":
                return embed_ready, at[0] + 1
            if kind == "qkv":
                m, c, group = at
                return sigmoid_ready, GROUPS * (DIM_CHUNKS * m + c) + order.index(group) + 1
            if kind == "absmean":
                return absmean_ready, 1
            if kind == "valueT":
                c, group = at
                return value_ready, GROUPS * c + order.index(group) + 1
            if kind == "gram":
                c, half = at
                return gram_ready, 2 * c + half + 1
            if kind == "ffn_rows":
                return row_parts_ready, 1
            if kind == "mix":
                c, group = at
                return att_lo_ready, DIM_CHUNKS * order.index(group) + c + 1
            if kind == "proj":
                return h2_ready, place_of(at[0]) // 2 + 1
            if kind in ("up", "up2"):
                return g_ready, place_of(at[0]) + 1
            if kind == "gT":
                c, group = at
                return gT_lo_ready, HIDDEN_CHUNKS * order.index(group) + c + 1
            return final_ready, place_of(at[0]) + 1

        def cols(group):
            return slice(GROUP * group, GROUP * (group + 1))

        def qkv_index(m, c):
            return DIM_CHUNKS * m + c

        blk = ctx.enter_context(nc.Block())

        @blk.sync
        def _(sp):
            def load_embed(f):
                sp.dma_start(embed[:, f, :], embed_in[:, f, :]).then_inc(embed_loaded[f], 16)

            def load_text(n):
                tiles = slice(GROUP_TILES * n, GROUP_TILES * (n + 1))
                sp.dma_start(h[:, GROUP_TILES * (n + 1):GROUP_TILES * (n + 2), :], text_in[:, tiles, :])\
                    .then_inc(text_loaded[n], 16)

            load_embed(0)
            load_embed(1)
            load_text(0)
            load_embed(2)
            load_text(1)
            load_embed(3)
            load_embed(4)
            sp.dma_start(squares[:, :], squares_in).then_inc(identity_loaded, 16)
            load_embed(5)
            sp.dma_start(w_qkv[:, :, 0:DIM], w_qkv_in[:, :, 0:DIM]).then_inc(w_v_loaded, 16)
            sp.dma_start(w_qkv[:, :, DIM:3 * DIM], w_qkv_in[:, :, DIM:3 * DIM]).then_inc(w_kq_loaded, 16)
            sp.dma_start(columns[:, :], columns_in).then_inc(constants_loaded, 16)
            sp.dma_start(proj_bias[:, :], proj_bias_in.partition_broadcast(P)).then_inc(constants_loaded, 16)
            sp.dma_start(w_up[:, :], w_up_in).then_inc(w_up_loaded, 16)
            sp.dma_start(w_down[:, :], w_down_in).then_inc(w_down_loaded, 16)
            sp.dma_start(w_proj[:, :, :], w_proj_in).then_inc(w_proj_loaded, 16)
            sp.wait_ge(row_parts_ready, 1)
            for r in range(4):
                row = row_parts[r:r + 1, :].rearrange("r (a d) -> r a d", a=1).broadcast_to([1, P, DIM])
                sp.dma_start(spread_parts[:, r, :], row).then_inc(rows_spread, 16)
            for n, t in enumerate(final_order):
                sp.wait_ge(final_ready, n + 1)
                sp.dma_start(out[t], h[:, t, :]).then_inc(out_stored, 16)
            sp.wait_ge(out_stored, 16 * TILES)

        @blk.tensor
        def _(pe):
            def claim(what):
                if BEFORE[what]:
                    pe.wait_ge(*was_read(BEFORE[what]))
                return psum[:, BANK[what], :]

            def matmuls(dst, pairs):
                for i, (stationary, moving) in enumerate(pairs):
                    last = pe.matmul(dst, stationary, moving, start=(i == 0), stop=(i == len(pairs) - 1))
                return last

            def transposes(what, sources):
                bank = claim(what)
                for i, source in enumerate(sources):
                    last = pe.transpose(bank[:, P * i:P * (i + 1)], source, identity)
                last.then_inc(bank_full[BANK[what]], 1)

            def transpose_xn(kind, k, group):
                what = (kind, k, group)
                bank = claim(what)
                done = TILES * (kind == "x2T") + GROUP_TILES * order.index(group)
                for i, t in enumerate(tiles_of(group)):
                    if k == 0:
                        pe.wait_ge(xn_ready, done + i + 1)
                    last = pe.transpose(bank[:, P * i:P * (i + 1)], xn[:, t, P * k:P * (k + 1)], identity)
                last.then_inc(bank_full[BANK[what]], 1)

            def qkv(m, c, group, lows_ready=None):
                what = ("qkv", m, c, group)
                bank = claim(what)
                e = slice(DIM * m + P * c, DIM * m + P * (c + 1))
                pairs = []
                for k in range(DIM_CHUNKS):
                    pairs += [(w_qkv_hi[:, k, e], xnT_hi[:, k, cols(group)]),
                              (w_qkv_lo[:, k, e], xnT_hi[:, k, cols(group)]),
                              (w_qkv_hi[:, k, e], xnT_lo[:, k, cols(group)])]
                for i, (stationary, moving) in enumerate(pairs):
                    if lows_ready is not None and i % 3 == 0:
                        pe.wait_ge(xT_lo_ready, lows_ready + i // 3 + 1)
                    last = pe.matmul(bank, stationary, moving, start=(i == 0), stop=(i == len(pairs) - 1))
                last.then_inc(bank_full[BANK[what]], 1)

            def value_transpose(c, group):
                pe.wait_ge(sigmoid_ready, GROUPS * c + order.index(group) + 1)
                transposes(("valueT", c, group),
                           [act_qkv[:, qkv_index(V, c), P * t:P * (t + 1)] for t in tiles_of(group)])

            def gram_product(c, half):
                what = ("gram", c, half)
                bank = claim(what)
                pe.wait_ge(value_ready, GROUPS * (c + 1))
                for i in range(4):
                    b = 4 * half + i
                    vt, vi = v_text[:, c, b, :], v_image[:, c, b % 2, b // 2, :]
                    last = matmuls(bank[:, P * i:P * (i + 1)], [(vt, vt), (vi, vi)])
                last.then_inc(bank_full[BANK[what]], 1)

            def mix(c, group):
                what = ("mix", c, group)
                bank = claim(what)
                qk = act_qkv[:, qkv_index(Q, c), :]
                if group:
                    batches, width, first = range(4 * (group - 1), 4 * group), TEXT_TOKENS, GROUP * group
                else:
                    batches, width, first = range(BATCHES), IMAGE_TOKENS, 0
                if group:
                    pe.wait_ge(qk_text_ready, 2 * c + order.index(group) + 1)
                else:
                    pe.wait_ge(qk_image_ready, c + 1)
                pe.wait_ge(gram_ready, 2 * c + (1 if group == order[0] else 2))
                for i, b in enumerate(batches):
                    last = pe.matmul(bank[:, width * i:width * (i + 1)], gram[:, c, b, :],
                                     qk[:, first + width * i:first + width * (i + 1)], start=True, stop=True)
                last.then_inc(bank_full[BANK[what]], 1)

            def proj(s, pair):
                t0 = GROUP_TILES * order[s] + 2 * pair
                what = ("proj", t0)
                bank = claim(what)
                for i in range(2):
                    at = slice(P * (t0 + i), P * (t0 + i + 1))
                    pairs = []
                    for c in range(DIM_CHUNKS):
                        pairs += [(attT_hi[:, c, at], w_proj_hi[:, c, :]),
                                  (attT_hi[:, c, at], w_proj_lo[:, c, :]),
                                  (attT_lo[:, c, at], w_proj_hi[:, c, :])]
                    last = matmuls(bank[:, DIM * i:DIM * (i + 1)], pairs)
                last.then_inc(bank_full[BANK[what]], 1)

            def up(t, lows_ready=None):
                claim(("up", t))
                claim(("up2", t))
                at = slice(P * t, P * (t + 1))
                for half in range(2):
                    bank = psum[:, BANK[("up", t)] + half, :]
                    for k in range(DIM_CHUNKS):
                        if lows_ready is not None and half == 0:
                            pe.wait_ge(xT_lo_ready, lows_ready + k + 1)
                        w = up_sign[:, HIDDEN * k + 512 * half:HIDDEN * k + 512 * (half + 1)]
                        pe.matmul(bank, x2T_hi[:, k, at], w, start=(k == 0), stop=False)
                        last = pe.matmul(bank, x2T_low[:, k, at], w, start=False, stop=(k == DIM_CHUNKS - 1))
                    last.then_inc(bank_full[BANK[("up", t)] + half], 1)

            def gT(s, c):
                transposes(("gT", c, order[s]),
                           [g[:, GROUP_TILES * (s % 2) + i, P * c:P * (c + 1)] for i in range(GROUP_TILES)])

            def down_pairs(s, i, c):
                w = down_sign[:, DIM * c:DIM * (c + 1)]
                at = slice(P * i, P * (i + 1))
                return [(gT_hi[s % 2][:, c, at], w), (gT_lo[s % 2][:, c, at], w)]

            def down(s, i):
                what = ("down", GROUP_TILES * order[s] + i)
                bank = claim(what)
                pe.wait_ge(gT_lo_ready, HIDDEN_CHUNKS * (s + 1))
                matmuls(bank[:, 0:DIM], [p for c in range(HIDDEN_CHUNKS) for p in down_pairs(s, i, c)])\
                    .then_inc(bank_full[BANK[what]], 1)

            pe.wait_ge(pool_constants, 2)
            for _ in range(WARM_UP_PRODUCTS):
                pe.matmul(psum[:, 7, 0:P], ones[:, :], ones[:, :], start=True, stop=True)
            for f in range(PATCH_CHUNKS):
                if f == PATCH_CHUNKS - 2:
                    pe.wait_ge(identity_loaded, 16)
                    for n in range(2):
                        for k in range(DIM_CHUNKS):
                            transpose_xn("xnT", k, order[n])
                if f in EMBED_SPLIT:
                    part = EMBED_SPLIT.index(f)
                    pe.wait_ge(embed_lo_ready, part + 1)
                    hi, lo = embed_hi[:, part, :], embed_lo[:, part, :]
                    operands = [(hi, hi), (hi, lo), (lo, hi)]
                else:
                    pe.wait_ge(embed_loaded[f], 16)
                    operands = [(embed[:, f, :], embed[:, f, :])]
                for t in range(IMAGE_TILES):
                    for n, (patches, weights) in enumerate(operands):
                        last = pe.matmul(psum[:, BANK[("embed", t)], 0:DIM], patches[:, P * t:P * (t + 1)],
                                         weights[:, GROUP:GROUP + DIM], start=(f == 0 and n == 0),
                                         stop=(f == PATCH_CHUNKS - 1 and n == len(operands) - 1))
                    if f == PATCH_CHUNKS - 1:
                        last.then_inc(bank_full[BANK[("embed", t)]], 1)
            first, second, image = order
            pe.wait_ge(w_qkv_lo_ready, 1)
            pe.wait_ge(xT_lo_ready, 2)
            qkv(V, 0, first)
            pe.wait_ge(xT_lo_ready, 4)
            qkv(V, 0, second)
            qkv(V, 1, first)
            for k in range(DIM_CHUNKS):
                transpose_xn("xnT", k, image)
            qkv(V, 1, second)
            qkv(V, 0, image, lows_ready=DIM_CHUNKS * 2)
            qkv(V, 1, image)
            pe.wait_ge(w_qkv_lo_ready, 2)
            qkv(K, 0, first)
            qkv(K, 0, second)
            qkv(K, 0, image)
            bank = claim(("absmean",))
            pe.wait_ge(abs_ready, 2)
            pe.matmul(bank[:, 0:2], ones[:, :], abs_sums[:, :], start=True, stop=True)\
                .then_inc(bank_full[BANK[("absmean",)]], 1)
            for group in order:
                qkv(K, 1, group)
            value_transpose(0, first)
            value_transpose(0, second)
            pe.wait_ge(w_qkv_lo_ready, 3)
            qkv(Q, 0, first)
            qkv(Q, 0, second)
            value_transpose(0, image)
            value_transpose(1, first)
            qkv(Q, 0, image)
            qkv(Q, 1, first)
            value_transpose(1, second)
            qkv(Q, 1, second)
            value_transpose(1, image)
            qkv(Q, 1, image)
            for c in range(DIM_CHUNKS):
                for half in range(2):
                    gram_product(c, half)

            def proj_group(s, pairs=(0, 1)):
                pe.wait_ge(w_proj_lo_ready, 1)
                pe.wait_ge(att_lo_ready, DIM_CHUNKS * (s + 1))
                for pair in pairs:
                    proj(s, pair)

            def x2T_group(s):
                for k in range(DIM_CHUNKS):
                    transpose_xn("x2T", k, order[s])

            def up_tile(s, i):
                up(GROUP_TILES * order[s] + i, lows_ready=DIM_CHUNKS * (GROUPS + s) if i == 0 else None)

            def gT_pair(s, i):
                if i == 0:
                    pe.wait_ge(g_ready, GROUP_TILES * (s + 1))
                gT(s, 2 * i)
                gT(s, 2 * i + 1)

            for group in (first, second):
                for c in range(DIM_CHUNKS):
                    mix(c, group)
            proj_group(0)
            for c in range(DIM_CHUNKS):
                mix(c, image)
            proj_group(1)
            proj_group(2, (0,))
            x2T_group(0)
            proj_group(2, (1,))
            bank = claim(("ffn_rows",))
            pe.wait_ge(row_weight_ready, 1)
            pe.wait_ge(down_ready, 4)
            matmuls(bank[0:4, 0:DIM], [(row_weights[:, c, :], down_sign[:, DIM * c:DIM * (c + 1)])
                                       for c in range(HIDDEN_CHUNKS)]).then_inc(bank_full[BANK[("ffn_rows",)]], 1)
            pe.wait_ge(up_ready, 2)
            up_tile(0, 0)
            up_tile(0, 1)
            x2T_group(1)
            up_tile(0, 2)
            up_tile(0, 3)
            up_tile(1, 0)
            for i in range(GROUP_TILES):
                gT_pair(0, i)
                if i + 1 < GROUP_TILES:
                    up_tile(1, i + 1)
                if i == 1:
                    x2T_group(2)
            up_tile(2, 0)
            for i in range(GROUP_TILES):
                gT_pair(1, i)
                if i + 1 < GROUP_TILES:
                    up_tile(2, i + 1)
                down(0, i)
            gT_pair(2, 0)
            for i in range(GROUP_TILES):
                if i + 1 < GROUP_TILES:
                    gT_pair(2, i + 1)
                down(1, i)
            for i in range(GROUP_TILES):
                down(2, i)

        @blk.scalar
        def _(act):
            def full(what):
                act.wait_ge(bank_full[BANK[what]], nth[what])
                return psum[:, BANK[what], :]

            def w_hi(m):
                e = slice(DIM * m, DIM * (m + 1))
                act.activation(w_qkv_hi[:, :, e], w_qkv[:, :, e], ACT.Copy).then_inc(w_qkv_hi_ready, 1)

            def xT_hi(kind, dst, k, group):
                act.activation(dst[:, k, cols(group)], full((kind, k, group)), ACT.Copy).then_inc(xT_hi_ready, 1)

            def sigmoids(m, c):
                j = qkv_index(m, c)
                act.wait_ge(bn_ready, j + 1)
                for group in order:
                    what = ("qkv", m, c, group)
                    act.activation(act_qkv[:, j, cols(group)], psum[:, BANK[what], :], ACT.Sigmoid,
                                   bias=bn_shift[:, j:j + 1], scale=bn_slope[:, j:j + 1])\
                        .then_inc(sigmoid_ready, 1)

            def values(c, group):
                bank = full(("valueT", c, group))
                which = BANK[("valueT", c, group)]
                if group:
                    act.activation(v_text[:, c, 4 * (group - 1):4 * group, :], bank, ACT.Copy)\
                        .then_inc(value_ready, 1)
                else:
                    act.activation(v_image[:, c, 0, :, :], bank, ACT.Identity, scale=half_mask[0])
                    act.activation(v_image[:, c, 1, :, :], bank, ACT.Identity, scale=half_mask[1])\
                        .then_inc(value_ready, 1)

            def att_hi(c, group):
                act.activation(attT_hi[:, c, cols(group)], full(("mix", c, group)), ACT.Copy).then_inc(att_hi_ready, 1)

            def gelu(s, i):
                t = GROUP_TILES * order[s] + i
                full(("up", t))
                full(("up2", t))
                bank = BANK[("up", t)]
                if s >= 2:
                    act.wait_ge(gT_lo_ready, HIDDEN_CHUNKS * (s - 1))
                    act.wait_ge(g_moment, GROUP_TILES * (s - 2) + i + 1)
                act.activation(g[:, GROUP_TILES * (s % 2) + i, :], psum[:, bank:bank + 2, :], ACT.Gelu)\
                    .then_inc(g_ready, 1)

            def g_hi(s, i):
                for c in (2 * i, 2 * i + 1):
                    act.activation(gT_hi[s % 2][:, c, :], full(("gT", c, order[s])), ACT.Copy, scale=ln_w[:, c:c + 1])\
                        .then_inc(gT_hi_ready, 1)

            first, second, image = order
            act.preload_act_table(ACT.Sigmoid)

            def split_embed(part):
                act.wait_ge(embed_loaded[EMBED_SPLIT[part]], 16)
                act.activation(embed_hi[:, part, :], embed[:, EMBED_SPLIT[part], :], ACT.Copy)\
                    .then_inc(embed_hi_ready, 1)

            for part in range(len(EMBED_SPLIT)):
                split_embed(part)
            for k in range(DIM_CHUNKS):
                xT_hi("xnT", xnT_hi, k, first)
            act.wait_ge(w_v_loaded, 16)
            w_hi(V)
            for k in range(DIM_CHUNKS):
                xT_hi("xnT", xnT_hi, k, second)
            for t in range(IMAGE_TILES):
                bank = full(("embed", t))
                act.activation(h[:, t, :], bank[:, 0:DIM], ACT.Copy).then_inc(embed_ready, 1)
            act.wait_ge(w_kq_loaded, 16)
            w_hi(K)
            w_hi(Q)
            act.wait_ge(constants_loaded, 32)
            act.activation(row_weights[:, :, 0:2], hidden_affine, ACT.Copy).then_inc(row_weight_hi_ready, 1)
            act.wait_ge(w_up_loaded, 16)
            act.activation(up_sign[:, :], w_up[:, :], ACT.Abs, accum_out=abs_sums[:, 0:1]).then_inc(abs_ready, 1)
            for k in range(DIM_CHUNKS):
                xT_hi("xnT", xnT_hi, k, image)
            act.wait_ge(w_down_loaded, 16)
            act.activation(down_sign[:, :], w_down[:, :], ACT.Abs, accum_out=abs_sums[:, 1:2]).then_inc(abs_ready, 1)
            act.wait_ge(w_proj_loaded, 16)
            act.activation(w_proj_hi[:, :, :], w_proj[:, :, :], ACT.Copy).then_inc(w_proj_hi_ready, 1)
            sigmoids(V, 0)
            sigmoids(V, 1)
            sigmoids(K, 0)
            values(0, first)
            values(0, second)
            sigmoids(K, 1)
            values(0, image)
            values(1, first)
            values(1, second)
            sigmoids(Q, 0)
            values(1, image)
            sigmoids(Q, 1)
            act.preload_act_table(ACT.Gelu)
            for group in order:
                for c in range(DIM_CHUNKS):
                    att_hi(c, group)
            for k in range(DIM_CHUNKS):
                xT_hi("x2T", x2T_hi, k, first)
            bank = full(("ffn_rows",))
            act.activation(row_parts[:, :], bank[0:4, 0:DIM], ACT.Copy, scale=row_sign).then_inc(row_parts_ready, 1)
            gelu(0, 0)
            gelu(0, 1)
            for k in range(DIM_CHUNKS):
                xT_hi("x2T", x2T_hi, k, second)
            gelu(0, 2)
            gelu(0, 3)
            gelu(1, 0)
            for i in range(GROUP_TILES):
                g_hi(0, i)
                if i + 1 < GROUP_TILES:
                    gelu(1, i + 1)
                if i == 1:
                    for k in range(DIM_CHUNKS):
                        xT_hi("x2T", x2T_hi, k, image)
            gelu(2, 0)
            for i in range(GROUP_TILES):
                g_hi(1, i)
                if i + 1 < GROUP_TILES:
                    gelu(2, i + 1)
            for i in range(GROUP_TILES):
                g_hi(2, i)

        @blk.gpsimd
        def _(pool):
            pool.memset(minus_half[:, :], -0.5).then_inc(pool_constants, 1)
            pool.memset(ones[:, :], 1.0).then_inc(pool_constants, 1)
            pool.wait_ge(pool_constants, 2)

            def norm_rsqrt(layer, n, group):
                pool.wait_ge(norm_var_ready, n)
                ts = slice(GROUP_TILES * group, GROUP_TILES * (group + 1))
                pool.tensor_tensor(norm_rstd[:, layer, ts], norm_var[:, layer, ts], minus_half[:, :], ALU.pow)\
                    .then_inc(norm_rstd_ready, 1)

            def bn_rsqrt(j):
                pool.wait_ge(bn_var_ready, j + 1)
                pool.tensor_tensor(bn_rstd[:, j:j + 1], bn_var[:, j:j + 1], minus_half[:, 0:1], ALU.pow)\
                    .then_inc(bn_rstd_ready, 1)

            def add_bias(n, group):
                pool.wait_ge(xn_ready, GROUP_TILES * (n + 1))
                for t in tiles_of(group):
                    pool.tensor_tensor(h[:, t, :], h[:, t, :], proj_bias[:, :], ALU.add).then_inc(biased, 1)

            def g_rsqrt(s):
                ts = slice(GROUP_TILES * order[s], GROUP_TILES * (order[s] + 1))
                pool.wait_ge(g_var_ready, s + 1)
                pool.tensor_tensor(g_rstd[:, ts], g_var[:, ts], minus_half[:, :], ALU.pow).then_inc(g_rstd_ready, 1)

            def shift_h2(s):
                pool.wait_ge(xn_ready, TILES + GROUP_TILES * (s + 1))
                pool.wait_ge(rows_ready, 1)
                for t in tiles_of(order[s]):
                    pool.tensor_tensor(h[:, t, :], h[:, t, :], rows[:, 1, :], ALU.add).then_inc(h2_shifted, 1)

            def subtract_mean(s):
                ts = slice(GROUP_TILES * order[s], GROUP_TILES * (order[s] + 1))
                pool.wait_ge(g_rstd_ready, s + 1)
                pool.tensor_tensor(g_mean_slope[:, ts], g_moments[:, ts, 0], g_rstd[:, ts], ALU.mult)\
                    .then_inc(g_mean_slope_ready, 1)
                pool.wait_ge(g_mean_slope_ready, s + 1)
                pool.wait_ge(h2_shifted, GROUP_TILES * (s + 1))
                for i, t in enumerate(tiles_of(order[s])):
                    n = GROUP_TILES * s + i
                    if n:
                        pool.wait_ge(h2_complete, n)
                    pool.tensor_scalar(row_term[:, :], rows[:, 0, :], g_mean_slope[:, t:t + 1], None, ALU.mult)\
                        .then_inc(row_term_ready, 1)
                    pool.wait_ge(row_term_ready, n + 1)
                    pool.tensor_tensor(h[:, t, :], h[:, t, :], row_term[:, :], ALU.add).then_inc(h2_complete, 1)

            def threshold_down(i):
                part = slice(512 * i, 512 * (i + 1))
                if i:
                    pool.wait_ge(down_ready, i)
                pool.tensor_scalar(positive[:, :], w_down[:, part], thresholds[:, 0, 1:2], None, ALU.is_gt)\
                    .then_inc(down_part, 1)
                pool.tensor_scalar(negative[:, :], w_down[:, part], thresholds[:, 1, 1:2], None, ALU.is_lt)\
                    .then_inc(down_part, 1)

            def ternary_down(i):
                part = slice(512 * i, 512 * (i + 1))
                pool.wait_ge(down_part, 2 * i + 2)
                pool.tensor_tensor(down_sign[:, part], positive[:, :], negative[:, :], ALU.subtract)\
                    .then_inc(down_ready, 1)

            norm_rsqrt(0, 1, 1)
            norm_rsqrt(0, 2, 2)
            for part, f in enumerate(EMBED_SPLIT):
                pool.wait_ge(embed_hi_ready, part + 1)
                pool.tensor_tensor(embed_lo[:, part, :], embed[:, f, :], embed_hi[:, part, :].bitcast(fp32),
                                   ALU.subtract).then_inc(embed_lo_ready, 1)
            norm_rsqrt(0, 3, 0)
            pool.wait_ge(constants_loaded, 32)
            add_bias(0, 1)
            add_bias(1, 2)
            bn_rsqrt(0)
            bn_rsqrt(1)
            add_bias(2, 0)
            bn_rsqrt(2)
            pool.wait_ge(threshold_ready, 2)
            threshold_down(0)
            bn_rsqrt(3)
            ternary_down(0)
            bn_rsqrt(4)
            threshold_down(1)
            bn_rsqrt(5)
            ternary_down(1)
            for c in range(DIM_CHUNKS):
                pool.wait_ge(sigmoid_ready, GROUPS * (qkv_index(Q, c) + 1))
                q = act_qkv[:, qkv_index(Q, c), cols(0)]
                pool.tensor_tensor(q, q, act_qkv[:, qkv_index(K, c), cols(0)], ALU.mult).then_inc(qk_image_ready, 1)
                threshold_down(2 + c)
                ternary_down(2 + c)
            for s in range(GROUPS):
                norm_rsqrt(1, GROUPS + s + 1, order[s])
            pool.wait_ge(rows_spread, 64)
            pool.tensor_tensor(rows[:, :, :], spread_parts[:, 0:2, :], spread_parts[:, 2:4, :], ALU.add)\
                .then_inc(rows_ready, 1)
            shift_h2(0)
            shift_h2(1)
            g_rsqrt(0)
            subtract_mean(0)
            shift_h2(2)
            g_rsqrt(1)
            subtract_mean(1)
            g_rsqrt(2)

        @blk.vector
        def _(dve):
            def full(what):
                dve.wait_ge(bank_full[BANK[what]], nth[what])
                return psum[:, BANK[what], :]

            def norm_statistics(layer, n, group, embedded=False):
                for i, t in enumerate(tiles_of(group)):
                    if embedded:
                        dve.wait_ge(embed_ready, i + 1)
                    dve.bn_stats(norm_stats[:, layer, t, :], h[:, t, :]).then_inc(norm_stat, 1)
                for i, t in enumerate(tiles_of(group)):
                    dve.wait_ge(norm_stat, GROUP_TILES * n + i + 1)
                    dve.bn_aggr(norm_moments[:, layer, t, :], norm_stats[:, layer, t, :]).then_inc(norm_moment, 1)
                dve.wait_ge(norm_moment, GROUP_TILES * (n + 1))
                ts = slice(GROUP_TILES * group, GROUP_TILES * (group + 1))
                dve.tensor_scalar(norm_var[:, layer, ts], norm_moments[:, layer, ts, 1], NORM_EPS, None, ALU.add)\
                    .then_inc(norm_var_ready, 1)

            def normalise(layer, n, group):
                dve.wait_ge(norm_rstd_ready, n + 1)
                for t in tiles_of(group):
                    dve.tensor_scalar(xn[:, t, :], h[:, t, :], norm_moments[:, layer, t, 0:1],
                                      norm_rstd[:, layer, t:t + 1], ALU.subtract, ALU.mult).then_inc(xn_ready, 1)

            def w_lo(m):
                e = slice(DIM * m, DIM * (m + 1))
                dve.wait_ge(w_qkv_hi_ready, m + 1)
                dve.tensor_tensor(w_qkv_lo[:, :, e], w_qkv[:, :, e], w_qkv_hi[:, :, e].bitcast(fp32), ALU.subtract)\
                    .then_inc(w_qkv_lo_ready, 1)

            def xT_lo(kind, hi, lo, n, k, group):
                dve.wait_ge(xT_hi_ready, n + 1)
                dve.tensor_tensor(lo[:, k, cols(group)], psum[:, BANK[(kind, k, group)], :],
                                  hi[:, k, cols(group)].bitcast(fp32), ALU.subtract)\
                    .then_inc(xT_lo_ready, 1)

            qkv_stats = []

            def qkv_statistics(m, c, group):
                j = qkv_index(m, c)
                dve.bn_stats(bn_stats[:, j, 6 * group:6 * (group + 1)], full(("qkv", m, c, group)))\
                    .then_inc(bn_stat, 1)
                qkv_stats.append((m, c, group))

            def qkv_affine(m, c):
                j = qkv_index(m, c)
                dve.wait_ge(bn_stat, len(qkv_stats))
                dve.bn_aggr(bn_moments[:, j, :], bn_stats[:, j, :]).then_inc(bn_moment, 1)
                dve.wait_ge(bn_moment, j + 1)
                dve.tensor_scalar(bn_var[:, j:j + 1], bn_moments[:, j, 1:2], NORM_EPS, None, ALU.add)\
                    .then_inc(bn_var_ready, 1)

            def qkv_affine_end(m, c):
                j = qkv_index(m, c)
                dve.wait_ge(bn_rstd_ready, j + 1)
                dve.tensor_tensor(bn_slope[:, j:j + 1], bn_rstd[:, j:j + 1], bn_gain[:, j:j + 1], ALU.mult)\
                    .then_inc(bn_slopes, 1)
                dve.tensor_tensor(bn_minus_slope[:, j:j + 1], bn_rstd[:, j:j + 1], bn_minus_gain[:, j:j + 1], ALU.mult)\
                    .then_inc(bn_slopes, 1)
                dve.wait_ge(bn_slopes, 2 * (j + 1))
                dve.scalar_tensor_tensor(bn_shift[:, j:j + 1], bn_moments[:, j, 0:1], bn_minus_slope[:, j:j + 1],
                                         bn_offset[:, j:j + 1], ALU.mult, ALU.add).then_inc(bn_ready, 1)

            def gram_scaled(c, half):
                what = ("gram", c, half)
                bank = full(what).rearrange("p (b e) -> p b e", b=4)
                mask = head_mask.rearrange("p (a e) -> p a e", a=1).broadcast_to([P, 4, P])
                dve.tensor_tensor(gram[:, c, 4 * half:4 * (half + 1), :], bank, mask, ALU.mult)\
                    .then_inc(gram_ready, 1)

            def att_lo(n, c, group):
                dve.wait_ge(att_hi_ready, n + 1)
                dve.tensor_tensor(attT_lo[:, c, cols(group)], psum[:, BANK[("mix", c, group)], :],
                                  attT_hi[:, c, cols(group)].bitcast(fp32), ALU.subtract)\
                    .then_inc(att_lo_ready, 1)

            def residual(s):
                for pair in range(2):
                    t0 = GROUP_TILES * order[s] + 2 * pair
                    what = ("proj", t0)
                    bank = full(what).rearrange("p (t d) -> p t d", t=2)
                    dve.tensor_tensor(h[:, t0:t0 + 2, :], bank, h[:, t0:t0 + 2, :], ALU.add)\
                        .then_inc(h2_ready, 1)
                dve.wait_ge(h2_ready, 2 * (s + 1))

            def second_norm(s):
                norm_statistics(1, GROUPS + s, order[s])

            def x2T_lo(s):
                for k in range(DIM_CHUNKS):
                    xT_lo("x2T", x2T_hi, x2T_low, DIM_CHUNKS * (GROUPS + s) + k, k, order[s])

            def g_statistics(s, i):
                t = GROUP_TILES * order[s] + i
                n = GROUP_TILES * s + i
                dve.wait_ge(g_ready, GROUP_TILES * s + i + 1)
                for half in range(2):
                    dve.bn_stats(g_stats[:, t, half, :], g[:, GROUP_TILES * (s % 2) + i, 512 * half:512 * (half + 1)])\
                        .then_inc(g_stat, 1)
                dve.wait_ge(g_stat, 2 * (n + 1))
                dve.bn_aggr(g_moments[:, t, :], g_stats[:, t, :, :].rearrange("p a b -> p (a b)")).then_inc(g_moment, 1)

                if i == GROUP_TILES - 1:
                    ts = slice(GROUP_TILES * order[s], GROUP_TILES * (order[s] + 1))
                    dve.wait_ge(g_moment, GROUP_TILES * (s + 1))
                    dve.tensor_scalar(g_var[:, ts], g_moments[:, ts, 1], NORM_EPS, None, ALU.add).then_inc(g_var_ready, 1)

            def g_lo(s, i):
                for c in (2 * i, 2 * i + 1):
                    dve.wait_ge(gT_hi_ready, HIDDEN_CHUNKS * s + c + 1)
                    what = ("gT", c, order[s])
                    dve.scalar_tensor_tensor(gT_lo[s % 2][:, c, :], psum[:, BANK[what], :], ln_w[:, c:c + 1],
                                             gT_hi[s % 2][:, c, :].bitcast(fp32), ALU.mult, ALU.subtract)\
                        .then_inc(gT_lo_ready, 1)

            def finish(s, i):
                t = GROUP_TILES * order[s] + i
                dve.wait_ge(h2_complete, GROUP_TILES * s + i + 1)
                dve.scalar_tensor_tensor(h[:, t, :], full(("down", t))[:, 0:DIM], g_rstd[:, t:t + 1], h[:, t, :],
                                         ALU.mult, ALU.add).then_inc(final_ready, 1)

            def subtract_last_mean():
                ts = slice(GROUP_TILES * order[-1], GROUP_TILES * (order[-1] + 1))
                dve.wait_ge(g_rstd_ready, GROUPS)
                dve.tensor_tensor(g_mean_slope[:, ts], g_moments[:, ts, 0], g_rstd[:, ts], ALU.mult)\
                    .then_inc(g_mean_slope_ready, 1)
                dve.wait_ge(g_mean_slope_ready, GROUPS)
                dve.wait_ge(h2_shifted, TILES)
                for t in tiles_of(order[-1]):
                    dve.scalar_tensor_tensor(h[:, t, :], rows[:, 0, :], g_mean_slope[:, t:t + 1], h[:, t, :],
                                             ALU.mult, ALU.add).then_inc(h2_complete, 1)

            first, second, image = order
            dve.wait_ge(text_loaded[0], 16)
            norm_statistics(0, 0, first)
            dve.wait_ge(text_loaded[1], 16)
            norm_statistics(0, 1, second)
            normalise(0, 0, first)
            normalise(0, 1, second)
            for k in range(DIM_CHUNKS):
                xT_lo("xnT", xnT_hi, xnT_lo, k, k, first)
            w_lo(V)
            for k in range(DIM_CHUNKS):
                xT_lo("xnT", xnT_hi, xnT_lo, DIM_CHUNKS + k, k, second)
            norm_statistics(0, 2, image, embedded=True)
            w_lo(K)
            normalise(0, 2, image)
            dve.wait_ge(constants_loaded, 32)
            dve.tensor_scalar(bn_gain[:, :], gain4, SIGMOID_SLOPE, None, ALU.mult).then_inc(bn_constants, 1)
            dve.tensor_scalar(bn_minus_gain[:, :], gain4, -SIGMOID_SLOPE, None, ALU.mult).then_inc(bn_constants, 1)
            dve.tensor_scalar(bn_offset[:, :], shift, V_THRESHOLD, SIGMOID_SLOPE, ALU.subtract, ALU.mult)\
                .then_inc(bn_constants, 1)
            qkv_statistics(V, 0, first)
            qkv_statistics(V, 0, second)
            for k in range(DIM_CHUNKS):
                xT_lo("xnT", xnT_hi, xnT_lo, 2 * DIM_CHUNKS + k, k, image)
            qkv_statistics(V, 1, first)
            dve.wait_ge(row_weight_hi_ready, 1)
            dve.tensor_tensor(row_weights[:, :, 2:4], hidden_affine, row_weights[:, :, 0:2].bitcast(fp32),
                              ALU.subtract).then_inc(row_weight_ready, 1)
            dve.wait_ge(bn_constants, 3)
            qkv_statistics(V, 0, image)
            qkv_affine(V, 0)
            qkv_statistics(V, 1, second)
            qkv_affine_end(V, 0)
            qkv_statistics(V, 1, image)
            qkv_affine(V, 1)
            qkv_statistics(K, 0, first)
            qkv_affine_end(V, 1)
            w_lo(Q)
            qkv_statistics(K, 0, second)
            qkv_statistics(K, 0, image)
            qkv_affine(K, 0)
            bank = full(("absmean",))
            dve.tensor_scalar(absmeans[:, :], bank[:, 0:2], 1.0 / (DIM * HIDDEN), ABSMEAN_EPS, ALU.mult, ALU.add)\
                .then_inc(absmean_ready, 1)
            qkv_affine_end(K, 0)
            dve.wait_ge(absmean_ready, 1)
            dve.tensor_scalar(thresholds[:, 0, :], absmeans[:, :], 0.5, None, ALU.mult).then_inc(threshold_ready, 1)
            dve.tensor_scalar(thresholds[:, 1, :], absmeans[:, :], -0.5, None, ALU.mult).then_inc(threshold_ready, 1)
            dve.wait_ge(w_proj_hi_ready, 1)
            dve.tensor_tensor(w_proj_lo[:, :, :], w_proj[:, :, :], w_proj_hi[:, :, :].bitcast(fp32), ALU.subtract)\
                .then_inc(w_proj_lo_ready, 1)
            for group in order:
                qkv_statistics(K, 1, group)
            qkv_affine(K, 1)
            qkv_affine_end(K, 1)
            dve.wait_ge(threshold_ready, 2)
            dve.tensor_scalar(up_negative[:, :], w_up[:, :], thresholds[:, 1, 0:1], None, ALU.is_lt)\
                .then_inc(up_part, 1)
            qkv_statistics(Q, 0, first)
            qkv_statistics(Q, 0, second)
            qkv_statistics(Q, 0, image)
            qkv_affine(Q, 0)
            qkv_affine_end(Q, 0)
            dve.wait_ge(up_part, 1)

            def ternary_up(k):
                part = slice(HIDDEN * k, HIDDEN * (k + 1))
                dve.scalar_tensor_tensor(up_sign[:, part], w_up[:, part], thresholds[:, 0, 0:1], up_negative[:, part],
                                         ALU.is_gt, ALU.subtract).then_inc(up_ready, 1)

            def query_key(c, group):
                dve.wait_ge(sigmoid_ready, GROUPS * qkv_index(Q, c) + order.index(group) + 1)
                q = act_qkv[:, qkv_index(Q, c), cols(group)]
                dve.tensor_tensor(q, q, act_qkv[:, qkv_index(K, c), cols(group)], ALU.mult).then_inc(qk_text_ready, 1)

            ternary_up(0)
            qkv_statistics(Q, 1, first)
            qkv_statistics(Q, 1, second)
            qkv_statistics(Q, 1, image)
            qkv_affine(Q, 1)
            qkv_affine_end(Q, 1)
            query_key(0, first)
            query_key(0, second)
            ternary_up(1)
            gram_scaled(0, 0)
            gram_scaled(0, 1)
            query_key(1, first)
            query_key(1, second)
            gram_scaled(1, 0)
            gram_scaled(1, 1)
            for n, group in enumerate((first, second)):
                for c in range(DIM_CHUNKS):
                    att_lo(DIM_CHUNKS * n + c, c, group)
            dve.wait_ge(biased, TILES)
            residual(0)
            second_norm(0)
            for c in range(DIM_CHUNKS):
                att_lo(2 * DIM_CHUNKS + c, c, image)
            normalise(1, GROUPS, order[0])
            residual(1)
            second_norm(1)
            x2T_lo(0)
            residual(2)
            normalise(1, GROUPS + 1, order[1])
            second_norm(2)
            g_statistics(0, 0)
            x2T_lo(1)
            normalise(1, GROUPS + 2, order[2])
            g_statistics(0, 1)
            g_statistics(0, 2)
            for s in range(GROUPS):
                for i in range(GROUP_TILES):
                    g_lo(s, i)
                    for n in STATISTICS_AFTER[s][i]:
                        g_statistics(n // GROUP_TILES, n % GROUP_TILES)
                    if s == 0 and i == 1:
                        x2T_lo(2)
                    if s == 1:
                        finish(0, i)
                    if s == 2 and i:
                        finish(1, i - 1)
            finish(1, GROUP_TILES - 1)
            subtract_last_mean()
            for i in range(GROUP_TILES):
                finish(GROUPS - 1, i)


_SHAPE = (TILES, P, DIM)


def kernel(**inputs):
    import concourse.bacc as _bacc
    from concourse.bass_utils import run_bass_kernel_spmd as _run

    a = {k: np.asarray(v) for k, v in inputs.items()}

    def feature_major(m, chunks):
        return np.ascontiguousarray(m.reshape(chunks, P, -1).transpose(1, 0, 2))

    side = a["x"].shape[1] // PATCH
    image = a["x"].reshape(BATCHES, side, PATCH, side, PATCH, 3).transpose(2, 4, 5, 0, 1, 3)
    image = image.reshape(PATCH_FEATURES, BATCHES * IMAGE_TOKENS)
    w_qkv = np.concatenate([a["L0_attn_Wv"].T, a["L0_attn_Wk"].T, a["L0_attn_Wq"].T], axis=1)
    halves = np.zeros((P, 2), np.float32)
    halves[:64, 0] = 1.0
    halves[64:, 1] = 1.0
    row_sign = np.ones((P, 1), np.float32)
    row_sign[0:4:2] = -1.0
    columns = np.concatenate(
        [a[f"L0_attn_{n}{m}"].reshape(2, P).T for n in "gb" for m in "vkq"]
        + [np.stack([a["L0_ffn_ln_w"], a["L0_ffn_ln_b"]], axis=1).reshape(HIDDEN_CHUNKS, P, 2).transpose(1, 0, 2)
           .reshape(P, -1), halves, row_sign], axis=1)
    head = np.arange(P) // HEAD_DIM
    squares = np.concatenate(
        [np.eye(P, dtype=np.float32),
         np.where(head[:, None] == head[None, :], np.float32(HEAD_DIM ** -0.5), np.float32(0))], axis=1)
    arrays = {
        "embed_in": np.concatenate([feature_major(image, PATCH_CHUNKS), feature_major(a["L0_tok_W"], PATCH_CHUNKS)],
                                   axis=2),
        "text_in": np.ascontiguousarray(a["txt"].transpose(1, 0, 2)),
        "w_qkv_in": feature_major(w_qkv, DIM_CHUNKS),
        "w_proj_in": feature_major(a["L0_attn_Wp"].T, DIM_CHUNKS),
        "w_up_in": feature_major(a["L0_ffn_W_fc"].T, DIM_CHUNKS).reshape(P, -1),
        "w_down_in": feature_major(a["L0_ffn_W_proj"].T, HIDDEN_CHUNKS).reshape(P, -1),
        "columns_in": np.ascontiguousarray(columns),
        "proj_bias_in": a["L0_attn_bp"],
        "squares_in": np.ascontiguousarray(squares),
    }
    nc = _bacc.Bacc("TRN2", target_bir_lowering=False, num_devices=1)
    args = {n: nc.dram_tensor(n, v.shape, mybir.dt.from_np(v.dtype), kind="ExternalInput").ap()
            for n, v in arrays.items()}
    out = nc.dram_tensor("out", _SHAPE, mybir.dt.float32, kind="ExternalOutput").ap()
    block(nc, *args.values(), out)
    r = _run(nc, [arrays], core_ids=[0]).results[0]["out"]
    result = np.empty((BATCHES, IMAGE_TOKENS + TEXT_TOKENS, DIM), r.dtype)
    result[:, :IMAGE_TOKENS] = r[:IMAGE_TILES].reshape(BATCHES, IMAGE_TOKENS, DIM)
    result[:, IMAGE_TOKENS:] = r[IMAGE_TILES:]
    return result
```
